# Optimizing a Trainium2 kernel written in Bass

```python
import numpy as np
import jax
import jax.numpy as jnp

def _softmax(x, axis=-1):
    return jax.nn.softmax(x, axis=axis)

def _gelu(x):
    return jax.nn.gelu(x, approximate=True)

def _silu(x):
    return jax.nn.silu(x)

def _sigmoid(x):
    return jax.nn.sigmoid(x)

def _layernorm(x, axis=-1, eps=1e-05):
    m = jnp.mean(x, axis=axis, keepdims=True)
    v = jnp.var(x, axis=axis, keepdims=True)
    return (x - m) / jnp.sqrt(v + eps)

def _scatter_add(tgt, idx, src, axis=0):
    return tgt.at[idx].add(src)

def _segment_sum(src, seg, n):
    return jax.ops.segment_sum(src, seg, n)
kernel_name = 'mk_decoder_preln_d1_seqx_r2_22664f'

def setup_inputs(seed: int=0):
    np.random.seed(seed)
    _w = jnp.asarray

    def _rec_inputs():
        import jax
        import jax.numpy as jnp
        _rk = jax.random.key(seed)
        x = 4.136e-05 + 0.9999 * jax.random.normal(jax.random.fold_in(_rk, 1), (8, 512, 512), jnp.float32)
        _lenS = 512 - jax.random.randint(jax.random.fold_in(_rk, 7), (8,), 0, max(1, 512 // 4) + 1, jnp.int32)
        _lenS2 = 512 - jax.random.randint(jax.random.fold_in(_rk, 8), (8,), 0, max(1, 512 // 4) + 1, jnp.int32)
        _ctx_2048P = jax.random.normal(jax.random.fold_in(_rk, 11), (8, 16, 1024), jnp.float32)
        _ctx_2048c = jax.random.dirichlet(jax.random.fold_in(_rk, 511), 0.3 * jnp.ones((16,), jnp.float32), (8, 512))
        _ctx_2048t = jnp.einsum('bsk,bkd->bsd', _ctx_2048c, _ctx_2048P)
        _ctx_2048t = _ctx_2048t * jax.lax.rsqrt(jnp.mean(jnp.square(_ctx_2048t)) + 1e-12) * 0.953939
        ctx_2048 = -0.000392918 + 0.999932 * (_ctx_2048t + 0.3 * jax.random.normal(jax.random.fold_in(_rk, 611), (8, 512, 1024), jnp.float32))
        itok_Bx1_68_817 = jax.random.randint(jax.random.fold_in(_rk, 12), (8, 1), 68, 409, jnp.int32)
        return (x, ctx_2048, itok_Bx1_68_817)
    x, ctx_2048, itok_Bx1_68_817 = _rec_inputs()

    def _L0_attn_setup():
        import jax, jax.numpy as jnp
        import numpy as np
        import math
        B, S, D, H = (4, 1024, 512, 16)
        DK = D // H
        key = jax.random.key(seed)
        ks = jax.random.split(key, 5)
        scale = 1.0 / math.sqrt(D)
        return {'x': jax.random.normal(ks[0], (B, S, D), dtype=jnp.float32), 'Wv': jax.random.normal(ks[1], (D, D), dtype=jnp.float32) * scale, 'bv': jax.random.normal(ks[2], (D,), dtype=jnp.float32) * scale, 'Wo': jax.random.normal(ks[3], (D, D), dtype=jnp.float32) * scale, 'bo': jax.random.normal(ks[4], (D,), dtype=jnp.float32) * scale}
    _L0_attn_all = _L0_attn_setup()
    _L0_attn_in = {k: v for k, v in _L0_attn_all.items() if k in ('Wv', 'bv', 'Wo', 'bo')}
    del _L0_attn_all

    def _L0_xattn_setup():
        import jax, jax.numpy as jnp
        import numpy as np
        UNITS = 512
        NUM_HEADS = 16
        MASK_VALUE = -1000000000000.0

        def _split_heads(x, n):
            B, S, D = x.shape
            return x.reshape(B, S, n, D // n).transpose(0, 2, 1, 3)
        key = jax.random.key(seed)
        k1, k2, k3, k4 = jax.random.split(key, 4)
        B, S = (8, 512)
        memory = jax.random.normal(k1, (B, S, 2 * UNITS), dtype=jnp.float32)
        query = jax.random.normal(k2, (B, S, UNITS), dtype=jnp.float32)
        b = jax.random.normal(k3, (S,), dtype=jnp.float32)
        seq_len = jax.random.randint(k4, (B, 1), 0, S, dtype=jnp.int32)
        return {'memory': memory, 'query': query, 'b': b, 'seq_len': seq_len}
    _L0_xattn_all = _L0_xattn_setup()
    _L0_xattn_in = {k: v for k, v in _L0_xattn_all.items() if k in ('b',)}
    del _L0_xattn_all

    def _L0_ffn_setup():
        import jax, jax.numpy as jnp
        import numpy as np
        DIM = 512
        HIDDEN = 1536
        SCALE = 1.0 / 127.0

        def _dequant(w_int, dtype):
            return w_int.astype(dtype) * jnp.asarray(SCALE, dtype)
        key = jax.random.key(seed)
        k_x, k_g, k_u, k_d = jax.random.split(key, 4)
        x = jax.random.normal(k_x, (4, 1024, DIM), dtype=jnp.float32)
        w_gate = jax.random.randint(k_g, (HIDDEN, DIM), -127, 128, dtype=jnp.int32)
        w_up = jax.random.randint(k_u, (HIDDEN, DIM), -127, 128, dtype=jnp.int32)
        w_down = jax.random.randint(k_d, (DIM, HIDDEN), -127, 128, dtype=jnp.int32)
        return {'x': x, 'w_gate': w_gate, 'w_up': w_up, 'w_down': w_down}
    _L0_ffn_all = _L0_ffn_setup()
    _L0_ffn_in = {k: v for k, v in _L0_ffn_all.items() if k in ('w_gate', 'w_up', 'w_down')}
    del _L0_ffn_all
    return {'x': x, 'ctx_2048': ctx_2048, 'itok_Bx1_68_817': itok_Bx1_68_817, 'L0_attn_Wv': _L0_attn_in['Wv'], 'L0_attn_bv': _L0_attn_in['bv'], 'L0_attn_Wo': _L0_attn_in['Wo'], 'L0_attn_bo': _L0_attn_in['bo'], 'L0_xattn_b': _L0_xattn_in['b'], 'L0_ffn_w_gate': _L0_ffn_in['w_gate'], 'L0_ffn_w_up': _L0_ffn_in['w_up'], 'L0_ffn_w_down': _L0_ffn_in['w_down']}

def reference(x, ctx_2048, itok_Bx1_68_817, L0_attn_Wv, L0_attn_bv, L0_attn_Wo, L0_attn_bo, L0_xattn_b, L0_ffn_w_gate, L0_ffn_w_up, L0_ffn_w_down):
    import jax
    import jax.numpy as jnp

    def _L0_attn_ref(x, Wv, bv, Wo, bo):
        import jax, jax.numpy as jnp
        import numpy as np
        import math
        B, S, D, H = (4, 1024, 512, 16)
        DK = D // H
        b, s, d = x.shape
        h, dk = (H, DK)
        p = jnp.einsum('bsd,ed->bse', x, Wv) + bv
        p = p.reshape(b, s, h, dk).transpose(0, 2, 1, 3)
        q = k = v = p
        scores = jnp.einsum('bhqd,bhkd->bhqk', q, k) / math.sqrt(dk)
        attn = jax.nn.softmax(scores, axis=-1)
        out = jnp.einsum('bhqk,bhkd->bhqd', attn, v)
        out = out.reshape(b, s, h * dk)
        return jnp.einsum('bsd,ed->bse', out, Wo) + bo

    def _L0_xattn_ref(memory, query, b, seq_len):
        import jax, jax.numpy as jnp
        import numpy as np
        UNITS = 512
        NUM_HEADS = 16
        MASK_VALUE = -1000000000000.0

        def _split_heads(x, n):
            B, S, D = x.shape
            return x.reshape(B, S, n, D // n).transpose(0, 2, 1, 3)
        B, S, _ = query.shape
        dh = UNITS // NUM_HEADS
        k_mem, v_mem = jnp.split(memory, 2, axis=2)
        Q = _split_heads(query, NUM_HEADS) * dh ** (-0.5)
        Kh = _split_heads(k_mem, NUM_HEADS)
        Vh = _split_heads(v_mem, NUM_HEADS)
        logits = jnp.einsum('bhqd,bhkd->bhqk', Q, Kh) + b
        valid = (jnp.arange(S)[None, :] < seq_len[:, 0:1]).astype(jnp.float32)
        logits = logits + MASK_VALUE * (1.0 - valid)[:, None, None, :]
        weights = jax.nn.softmax(logits, axis=-1)
        out = jnp.einsum('bhqk,bhkd->bhqd', weights, Vh)
        return out.transpose(0, 2, 1, 3).reshape(B, S, UNITS)

    def _L0_ffn_ref(x, w_gate, w_up, w_down):
        import jax, jax.numpy as jnp
        import numpy as np
        DIM = 512
        HIDDEN = 1536
        SCALE = 1.0 / 127.0

        def _dequant(w_int, dtype):
            return w_int.astype(dtype) * jnp.asarray(SCALE, dtype)
        wg = _dequant(w_gate, x.dtype)
        wu = _dequant(w_up, x.dtype)
        wd = _dequant(w_down, x.dtype)
        gate = jnp.einsum('bsd,hd->bsh', x, wg)
        up = jnp.einsum('bsd,hd->bsh', x, wu)
        h = jax.nn.silu(gate) * up
        return jnp.einsum('bsh,dh->bsd', h, wd)
    x = x + _L0_attn_ref(_layernorm(x, axis=-1), L0_attn_Wv, L0_attn_bv, L0_attn_Wo, L0_attn_bo)
    x = x + _L0_xattn_ref(ctx_2048, _layernorm(x, axis=-1), L0_xattn_b, itok_Bx1_68_817)
    x = x + _L0_ffn_ref(_layernorm(x, axis=-1), L0_ffn_w_gate, L0_ffn_w_up, L0_ffn_w_down)
    return x

_drawn_inputs = setup_inputs


def setup_inputs(seed=0):
    import zlib

    import numpy as np

    out = dict(_drawn_inputs(seed))
    spreads = {}
    factors = {}
    for name, (base, spread) in spreads.items():
        noise = np.random.default_rng([zlib.crc32(name.encode()), seed]).standard_normal(out[name].shape)
        drawn = base * np.exp(spread * noise) if base else spread * noise
        out[name] = jnp.asarray(drawn.astype(out[name].dtype))
    for name, factor in factors.items():
        out[name] = (out[name] * factor).astype(out[name].dtype)
    return out
```

```python
from contextlib import ExitStack

import numpy as np

import concourse.bass as bass
from concourse import mybir

F32 = mybir.dt.float32
F16 = mybir.dt.float16
I32 = mybir.dt.int32
ALU = mybir.AluOpType
ACT = mybir.ActivationFunctionType
AX_X = mybir.AxisListType.X

P = 128
B, S, D, H = 8, 512, 512, 16
DH = D // H
T = S // P
KD = D // P
G = 4
HG = H // G
HID = 1536
MH = HID // P
HALF = S // 2
EPS = 1e-5

SX = 1024.0
SW = 64.0
SP_ = 16.0
SHID = 0.125
DEQ = 1.0 / 127.0
CA_SCORE = SX * SP_
SHIFT_SA, SHIFT_CA = 1024.0, 16384.0
SA, CA = 0, 1
K_MAX = {SA: 3 * DH, CA: 3 * DH + 3}
SHIFT_ROW = {SA: 3 * DH, CA: 3 * DH + 3}
USES = 2 * G
UNITS = T * HG


class At:

    def __init__(self, reg, off=0):
        self.reg, self.off = reg, off

    def plus(self, n):
        return At(self.reg, self.off + n)

    def count(self, per_batch, within):
        fixed = self.off * per_batch + within
        return fixed if self.reg is None else self.reg * per_batch + fixed

    def index(self):
        return self.off if self.reg is None else self.reg + self.off


class Work:

    def __init__(self, steps, before, first):
        self.number, self.before, self.first = {}, before, first
        for step in steps:
            for key in work_units(step):
                self.number[key] = len(self.number)
        self.units = len(self.number)

    def bank(self, key):
        return self.number[key] % 2

    def released(self, key, at):
        n = self.before + self.number[key]
        base = n // 2 + 1
        return at.plus(-self.first).count(self.units // 2, base)

    def free(self, key, at):
        n = self.before + self.number[key]
        return at.plus(-self.first).count(self.units // 2, n // 2)


def work_units(step):
    kind = step[0]
    if kind == "norm":
        return [("norm",) + step[1:]]
    if kind in ("proj", "proj_t", "out_proj", "shift", "denom", "gate_up", "down"):
        return [step]
    if kind == "back":
        return [("back_d", step[1]), ("back_o", step[1])]
    return []


def norm_pieces(ln, tiles):
    out = [[("stats", ln, t)] for t in tiles] + [[("rstd", ln, tiles)]]
    return out + [[("norm", ln, t), ("norm_lo", ln, t)] for t in tiles]


def project_pieces():
    out = norm_pieces(1, [0, 1, 2, 3]) + [[("load_x",)], [("add_bo",)]]
    out += [[("proj", t)] for t in range(T)]
    return out + [[("proj_t", g), ("proj_lo", g)] for g in range(G)] + [[("stack_proj",)]]


def attention_steps(x, fill):
    out = [("maxima", x, 0, j) for j in range(HG)]
    for g in range(G):
        out += fill()
        out.append(("shift", x, g))
        out += fill()
        for kt in range(T):
            if g + 1 < G:
                out.append(("maxima", x, g + 1, kt))
            if g and kt == T - 1:
                out.append(("denom", x, g - 1))
            out.append(("probs", x, g, kt))
            if kt:
                out.append(("values", x, g, kt - 1))
            if g and kt == T - 1:
                out.append(("finish", x, g - 1))
        out.append(("values", x, g, T - 1))
        if g and x == CA:
            out.append(("back", g - 1))
        if x == SA:
            out.append(("keys", g))
    if x == SA:
        out.append(("stack_keys",))
    out += fill()
    out.append(("denom", x, G - 1))
    out.append(("finish", x, G - 1))
    if x == CA:
        out.append(("back", G - 1))
    return out


def mlp_pieces(hf):
    out = norm_pieces(3, [2 * hf, 2 * hf + 1])
    out += [[("gate_up", hf, m)] for m in range(MH)]
    out.append([("hidden_end", hf)])
    return out + [[("down", hf, t)] for t in (2 * hf, 2 * hf + 1)]


def spread(pieces, n):
    shares = [sum(pieces[len(pieces) * i // n:len(pieces) * (i + 1) // n], []) for i in range(n)]

    def fill():
        return shares.pop(0) if shares else []
    return fill


def alone(pieces):
    out, late = [], []
    for p in pieces:
        out += p[:1] + late if len(p) > 1 else late + p
        late = p[1:]
    return out + late


def weave(pieces, fill):
    out, n = [], 0
    for i, p in enumerate(pieces):
        due = (i + 1) * len(fill) // len(pieces)
        out += p[:1]
        if len(p) > 1 and n < due:
            out += fill[n]
            n += 1
        out += p[1:]
        out += sum(fill[n:due], [])
        n = due
    return out


MID_LEAVES = 4


def batch_steps(first, last):
    beside = [[("weights", c)] for c in range(MH)] if first else mlp_pieces(1)
    late = 0 if first else len(beside) - MID_LEAVES
    out = attention_steps(SA, spread(beside[:len(beside) - late], 9))
    if not last:
        out.insert(0, ("load_ordered",))
    mid = [[("out_proj", t)] for t in range(T)] + norm_pieces(2, [0, 1, 2, 3]) + [[("queries",)]]
    out += weave(mid, beside[len(beside) - late:]) if late else alone(mid)
    out += attention_steps(CA, lambda: [])
    out.append(("residual",))
    if last:
        return out + alone(mlp_pieces(0))
    return out + weave([[("load_v",)]] + project_pieces(), mlp_pieces(0))


def build(nc, x, ctx, ctx_kT, lens, wvT, bv, woT, bo, key_bias, wgT, wuT, wdT, positions, row_consts, out):
    plans = {}
    order = []
    before = 0
    for name, steps, first in (
            ("start", alone(project_pieces()), -1),
            ("batch0", batch_steps(True, False), 0),
            ("loop", batch_steps(False, False), 1),
            ("last", batch_steps(False, True), B - 1),
            ("tail", alone(mlp_pieces(1)), B)):
        w = Work(steps, before, first)
        plans[name] = (steps, w)
        order.append(name)
        assert w.units % 2 == 0
        before += w.units * (B - 2 if name == "loop" else 1)

    with ExitStack() as es:
        def sb(name, shape, dt):
            return es.enter_context(nc.sbuf_tensor(name, shape, dt))

        def ps(name, shape):
            return es.enter_context(nc.psum_tensor(name, shape, F32))

        def sem(name):
            return es.enter_context(nc.semaphore(name))

        wv = sb("wv", [P, 2, KD, D], F16)
        wo = sb("wo", [P, 2, KD, D], F16)
        wg = sb("wg", [P, KD, HID], F16)
        wu = sb("wu", [P, KD, HID], F16)
        wd = sb("wd", [P, MH, D], F16)
        probs = sb("probs", [P, T, HG, S], F32)
        q_stack = sb("q_stack", [P, G, HG, S], F16)
        k_stack = sb("k_stack", [P, G, HG, S], F16)
        xin = sb("xin", [P, T, D], F32)
        res1 = sb("res1", [P, T, D], F32)
        res2 = sb("res2", [P, T, D], F32)
        xn = sb("xn", [P, 4, D], F32)
        actT = sb("actT", [P, 2, KD, S], F16)
        x3T = sb("x3T", [P, 2, KD, HALF], F16)
        hid = sb("hid", [P, 2, MH, HALF], F16)
        v_self = sb("v_self", [P, T, D], F32)
        v_ctx = sb("v_ctx", [P, T, D], F32)
        pqT = sb("pqT", [P, 2, KD, S], F16)
        keyT = sb("keyT", [P, S], F32)
        bvb = sb("bvb", [P, D], F32)
        bob = sb("bob", [P, D], F32)
        attn_raw = sb("attn_raw", [P, 2, S], F32)
        den = sb("den", [P, S], F32)
        attn_div = sb("attn_div", [P, S], F32)
        th = sb("th", [P, 2, HALF], F32)
        hraw = sb("hraw", [P, 2, HALF], F32)
        shift_row = sb("shift_row", [HG, S], F16)
        ident = sb("ident", [P, P], F32)
        ones = sb("ones", [P, DH], F32)
        negmax = sb("negmax", [P, 2, T, HG], F32)
        rcol = sb("rcol", [P, T * HG], F32)
        carrier = sb("carrier", [P, 1], F32)
        bst = sb("bst", [P, 3, T, 6], F32)
        mv = sb("mv", [P, 3, T, 2], F32)
        rs = sb("rs", [P, 3, T], F32)
        powers = sb("powers", [P, 2, T], F32)
        gate = sb("gate", [P, B], F32)
        lens_i = sb("lens_i", [P, B], I32)
        wv_raw = probs[:, 0]
        wo_raw = probs[:, 1]
        w_raw = hid[:].rearrange("p a m s -> p (a m s)").bitcast(I32).rearrange("p (c n) -> p c n", c=2)
        pos8 = probs[0:B, 2, 0]
        bias8 = probs[0:B, 2, 1]
        inv8 = probs[0:B, 2, 2]
        len8f = probs[0:B, 3, 0, 0:1]
        gate8 = probs[0:B, 3, 0, 1:2]
        len8i = probs[0:B, 3, 1, 0:1].bitcast(I32)
        rows8 = probs[0:B, 3, 2:4].rearrange("p a s -> p (a s)").bitcast(F16).rearrange(
            "p (r s) -> p r s", s=S)[:, 0:3]

        score_b = ps("score_b", [P, 3, S])
        score_a = ps("score_a", [P, 2, S])
        attn = ps("attn", [P, S])
        work = ps("work", [P, 2, S])

        key_rows = nc.dram_tensor("key_rows", [B, 3, S], F16, kind="Internal").ap()

        x_in = sem("x_in")
        xin_in = sem("xin_in")
        v_in = sem("v_in")
        key_in = sem("key_in")
        q_stacked = sem("q_stacked")
        k_stacked = sem("k_stacked")
        shift_in = sem("shift_in")
        stored = sem("stored")
        consts_in = sem("consts_in")
        wraw_in = [sem("wraw_in0"), sem("wraw_in1")]
        rows_out = sem("rows_out")
        row99_in = sem("row99_in")
        consts_made = sem("consts_made")
        table_step = sem("table_step")
        w_hi = sem("w_hi")
        w_lo = sem("w_lo")
        w_int = sem("w_int")
        work_free = [sem("work_free0"), sem("work_free1")]
        stat = {ln: sem(f"stat{ln}") for ln in (1, 2, 3)}
        meanvar = {ln: sem(f"meanvar{ln}") for ln in (1, 2, 3)}
        rstd = {ln: sem(f"rstd{ln}") for ln in (1, 2, 3)}
        normed = {ln: sem(f"normed{ln}") for ln in (1, 2, 3)}
        norm_t = {ln: sem(f"norm_t{ln}") for ln in (1, 2, 3)}
        norm_hi = {ln: sem(f"norm_hi{ln}") for ln in (1, 2, 3)}
        bo_added = sem("bo_added")
        proj_done = sem("proj_done")
        projt_done = sem("projt_done")
        projt_hi = sem("projt_hi")
        a_filled = sem("a_filled")
        max_done = sem("max_done")
        shift_t = sem("shift_t")
        b_filled = sem("b_filled")
        exp_done = sem("exp_done")
        values_done = sem("values_done")
        attn_out = sem("attn_out")
        sums = sem("sums")
        denom_done = sem("denom_done")
        div_done = sem("div_done")
        div_hi = sem("div_hi")
        div_used = sem("div_used")
        outproj_done = sem("outproj_done")
        key_hi = sem("key_hi")
        key_lo = sem("key_lo")
        back_d = sem("back_d")
        back_o = sem("back_o")
        moved = sem("moved")
        gu_filled = sem("gu_filled")
        tanh_done = sem("tanh_done")
        silu_done = sem("silu_done")
        hid_hi = sem("hid_hi")
        hid_lo = sem("hid_lo")
        down_done = sem("down_done")

        Q_PARTS = (0, 0, 1)
        K_PARTS = (0, 1, 0)
        BLOCKS = 16 * 3 * HG

        def q_ready(x_, at):
            return q_stacked, at.count(2 * BLOCKS + 16, BLOCKS if x_ == SA else 2 * BLOCKS + 16)

        def k_ready(x_, at):
            return k_stacked, at.count(2 * BLOCKS + 16 * 5, BLOCKS + 16 if x_ == SA else 2 * BLOCKS + 16 * 5)

        def need(eng, s, value):
            if not isinstance(value, int) or value > 0:
                eng.wait_ge(s, value)

        def walk(eng, do):
            for name in order:
                steps, w = plans[name]
                if name == "loop":
                    with eng.Fori(1, B - 1) as b:
                        for step in steps:
                            do(step, At(b), w)
                else:
                    for step in steps:
                        do(step, At(None, w.first), w)

        def mlp_at(hf, at):
            return at if hf == 0 else at.plus(-1)

        def ln_at(ln, t, at):
            return {1: at.plus(1), 2: at, 3: mlp_at(t // 2, at)}[ln]

        def folded(part, g):
            return actT[:, part, :, P * g:P * (g + 1)].rearrange("p k (j b) -> p j k b", j=HG)

        block = es.enter_context(nc.Block())

        @block.sync
        def _(sp):
            def load_ordered(xb):
                rows = xb.rearrange("(b k j) d -> k b j d", k=KD, j=T)
                for k in range(KD):
                    sp.dma_start(xin[DH * k:DH * (k + 1)], rows[k]).then_inc(xin_in, 16)

            load_ordered(x[0])
            sp.dma_start(res1[:], x[0].rearrange("(t p) d -> p t d", p=P)).then_inc(x_in, 16)
            sp.dma_start(wv_raw, wvT.rearrange("(k p) e -> p k e", p=P)).then_inc(wraw_in[0], 16)
            sp.dma_start(bvb[:], bv.rearrange("(o d) -> o d", o=1).broadcast_to([P, D])).then_inc(consts_in, 16)
            sp.dma_start(bob[:], bo.rearrange("(o d) -> o d", o=1).broadcast_to([P, D])).then_inc(consts_in, 16)
            sp.dma_start(pos8, positions.broadcast_to([B, S])).then_inc(consts_in, 16)
            sp.dma_start(bias8, key_bias.rearrange("(o d) -> o d", o=1).broadcast_to([B, S])).then_inc(consts_in, 16)
            sp.dma_start(len8i, lens).then_inc(consts_in, 16)
            sp.dma_start(lens_i[:], lens.rearrange("b o -> o b").broadcast_to([P, B])).then_inc(consts_in, 16)
            sp.dma_start(wo_raw, woT.rearrange("(k p) e -> p k e", p=P)).then_inc(wraw_in[1], 16)
            sp.dma_start(k_stack[99:100], row_consts[3:4].rearrange("r (g j s) -> r g j s", g=G, j=HG)
                         ).then_inc(row99_in, 16)
            sp.dma_start(v_ctx[:], ctx[0, :, D:2 * D].rearrange("(t p) d -> p t d", p=P)).then_inc(v_in, 16)
            sp.wait_ge(table_step, 9)
            sp.dma_start(key_rows, rows8).then_inc(rows_out, 16)
            sp.wait_ge(rows_out, 16)

            def load_keys(at, g):
                sp.dma_start(keyT[:], ctx_kT[bass.ds(at.index(), 1), P * g:P * (g + 1), :].rearrange(
                    "o e s -> (o e) s")).then_inc(key_in, 16)

            load_keys(At(None, 0), 0)

            def fill_stack(stack, parts, done):
                for j in range(HG):
                    for r, part in enumerate(parts):
                        sp.dma_start(stack[DH * r:DH * (r + 1), :, j, :],
                                     pqT[DH * j:DH * (j + 1), part]).then_inc(done, 16)

            def do(step, at, w):
                kind = step[0]
                if kind == "load_x" and not (at.reg is None and at.off == -1):
                    sp.wait_ge(moved, at.count(1, 1))
                    sp.dma_start(res1[:], x[bass.ds(at.plus(1).index(), 1)].rearrange(
                        "o (t p) d -> p (o t) d", p=P)).then_inc(x_in, 16)
                elif kind == "load_ordered" and not (at.reg is None and at.off == -1):
                    sp.wait_ge(normed[1], at.count(T, T))
                    load_ordered(x[bass.ds(at.plus(1).index(), 1)].rearrange("o s d -> (o s) d"))
                elif kind == "load_v":
                    sp.wait_ge(values_done, at.count(USES * T, USES * T))
                    sp.dma_start(v_ctx[:], ctx[bass.ds(at.plus(1).index(), 1), :, D:2 * D].rearrange(
                        "o (t p) d -> p (o t) d", p=P)).then_inc(v_in, 16)
                elif kind == "stack_proj":
                    need(sp, b_filled, at.count(USES * UNITS, USES * UNITS))
                    sp.dma_start(k_stack[96:97], row_consts[0:1].rearrange("r (g j s) -> r g j s", g=G, j=HG)
                                 ).then_inc(k_stacked, 16)
                    key = ("proj_t", G - 1)
                    sp.wait_ge(work_free[w.bank(key)], w.released(key, at))
                    fill_stack(k_stack, K_PARTS, k_stacked)
                    fill_stack(q_stack, Q_PARTS, q_stacked)
                elif kind == "shift":
                    _, x_, g = step
                    sp.wait_ge(work_free[w.bank(step)], w.released(step, at))
                    row = SHIFT_ROW[x_]
                    sp.dma_start(q_stack[row:row + 1, g, :, :], shift_row[:, :]).then_inc(shift_in, 16)
                elif kind == "keys":
                    g = step[1]
                    sp.wait_ge(key_lo, at.count(G, g + 1))
                    nb, ng = (at, g + 1) if g + 1 < G else (at.plus(1), 0)
                    if nb.reg is not None or nb.off < B:
                        load_keys(nb, ng)
                elif kind == "stack_keys":
                    sp.wait_ge(b_filled, at.count(USES * UNITS, G * UNITS))
                    fill_stack(k_stack, K_PARTS, k_stacked)
                    for g in range(G):
                        sp.dma_start(k_stack[96:99, g, :, :], key_rows[bass.ds(at.index(), 1)].rearrange(
                            "o r s -> (o r) s").unsqueeze(1).broadcast_to([3, HG, S])).then_inc(k_stacked, 16)
                elif kind == "queries":
                    key = ("norm", 2, T - 1)
                    sp.wait_ge(work_free[w.bank(key)], w.released(key, at))
                    fill_stack(q_stack, Q_PARTS, q_stacked)
                    sp.dma_start(q_stack[96:99], row_consts[0:3].rearrange("r (g j s) -> r g j s", g=G, j=HG)
                                 ).then_inc(q_stacked, 16)
                elif kind == "down":
                    _, hf, t = step
                    sp.wait_ge(work_free[w.bank(step)], w.released(step, at))
                    sp.dma_start(out.rearrange("b s d -> (b s) d")[bass.ds(mlp_at(hf, at).count(S, P * t), P), :],
                                 res2[:, t, :]).then_inc(stored, 16)
                elif kind == "weights":
                    c = step[1]
                    need(sp, w_int, c - 1)
                    src, k = divmod(c, KD)
                    if src < 2:
                        sp.dma_start(w_raw[:, c % 2], (wgT, wuT)[src][P * k:P * (k + 1), :]).then_inc(wraw_in[c % 2], 16)
                    else:
                        sp.dma_start(w_raw[:, c % 2].rearrange("p (m n) -> p m n", n=D),
                                     wdT[3 * P * k:3 * P * (k + 1), :].rearrange("(m p) n -> p m n", p=P)
                                     ).then_inc(wraw_in[c % 2], 16)
            walk(sp, do)
            sp.wait_ge(stored, 16 * T * B)
            sp.wait_ge(rows_out, 16)

        @block.tensor
        def _(pe):
            pe.wait_ge(consts_made, 6)
            pe.wait_ge(row99_in, 16)

            def do(step, at, w):
                kind = step[0]

                def claim(key):
                    need(pe, work_free[w.bank(key)], w.free(key, at))
                    return work[:, w.bank(key), :]

                def written(keys, claimed):
                    last = {w.bank(k): k for k in keys}
                    for bank, k in last.items():
                        if bank != w.bank(claimed):
                            pe.wait_ge(work_free[bank], w.released(k, at))

                if kind == "norm":
                    _, ln, t = step
                    bank = claim(step)
                    la = ln_at(ln, t, at)
                    pe.wait_ge(normed[ln], la.count(T, t + 1))
                    for k in range(KD):
                        last = nc.tensor.transpose(bank[:, P * k:P * (k + 1)], xn[:, t % 2 + 2 * (ln == 3), P * k:P * (k + 1)], ident[:])
                    last.then_inc(norm_t[ln], 1)
                elif kind == "proj":
                    t = step[1]
                    bank = claim(step)
                    if t == 0:
                        need(pe, w_lo, 1)
                    written([("norm", 1, t)], step)
                    n = 0
                    for k in range(KD):
                        for a, c in ((0, 0), (0, 1), (1, 0)):
                            last = nc.tensor.matmul(bank, actT[:, a, k, P * t:P * (t + 1)], wv[:, c, k, :],
                                                    start=n == 0, stop=n == 3 * KD - 1)
                            n += 1
                    last.then_inc(proj_done, 1)
                elif kind == "proj_t":
                    g = step[1]
                    bank = claim(step)
                    if g == 0:
                        written([("proj", T - 1)], step)
                    for t in range(T):
                        last = nc.tensor.transpose(bank[:, P * t:P * (t + 1)], v_self[:, t, P * g:P * (g + 1)], ident[:])
                    last.then_inc(projt_done, 1)
                elif kind == "maxima":
                    _, x_, g, j = step
                    u = G * x_ + g
                    rows = K_MAX[x_]
                    if g == 0 and j == 0:
                        pe.wait_ge(*q_ready(x_, at))
                        pe.wait_ge(*k_ready(x_, at))
                    for t in range(T):
                        n = u * UNITS + j * T + t
                        need(pe, max_done, at.count(USES * UNITS, n - 1))
                        nc.tensor.matmul(score_a[:, n % 2, :], q_stack[0:rows, g, j, P * t:P * (t + 1)],
                                         k_stack[0:rows, g, j, :], start=True, stop=True).then_inc(a_filled, 1)
                elif kind == "shift":
                    _, x_, g = step
                    u = G * x_ + g
                    bank = claim(step)
                    pe.wait_ge(max_done, at.count(USES * UNITS, (u + 1) * UNITS))
                    for t in range(T):
                        last = nc.tensor.transpose(bank[0:HG, P * t:P * (t + 1)], negmax[:, g % 2, t, :], ident[:])
                    last.then_inc(shift_t, 1)
                elif kind == "probs":
                    _, x_, g, kt = step
                    u = G * x_ + g
                    rows = SHIFT_ROW[x_] + 1
                    if kt == 0:
                        pe.wait_ge(shift_in, at.count(16 * USES, 16 * (u + 1)))
                    for j in range(HG):
                        r = kt * HG + j
                        prev = u * UNITS + r - 2 if r >= 3 else (u - 1) * UNITS + (16, 14, 15)[r]
                        need(pe, exp_done, at.count(USES * UNITS, prev))
                        nc.tensor.matmul(score_b[:, r % 3, :], k_stack[0:rows, g, j, P * kt:P * (kt + 1)],
                                         q_stack[0:rows, g, j, :], start=True, stop=True).then_inc(b_filled, 1)
                elif kind == "values":
                    _, x_, g, kt = step
                    u = G * x_ + g
                    v = v_self if x_ == SA else v_ctx
                    if kt == 0:
                        need(pe, attn_out, at.count(USES, u))
                        if x_ == CA and g == 0:
                            pe.wait_ge(v_in, at.count(16, 16))
                    pe.wait_ge(exp_done, at.count(USES * UNITS, u * UNITS + (kt + 1) * HG))
                    for j in range(HG):
                        h = g * HG + j
                        if x_ == CA:
                            last = nc.tensor.matmul(attn[DH * j:DH * (j + 1), :], v[:, kt, DH * h:DH * (h + 1)],
                                                    probs[:, kt, j, :], start=kt == 0, stop=kt == T - 1)
                        else:
                            for i in range(T):
                                last = nc.tensor.matmul(attn[DH * i:DH * (i + 1), P * j:P * (j + 1)],
                                                        v[:, kt, DH * h:DH * (h + 1)],
                                                        probs[:, kt, j, P * i:P * (i + 1)],
                                                        start=kt == 0 and j == 0, stop=kt == T - 1 and j == HG - 1,
                                                        skip_group_check=True)
                    last.then_inc(values_done, 1)
                elif kind == "denom":
                    _, x_, g = step
                    u = G * x_ + g
                    bank = claim(step)
                    pe.wait_ge(sums, at.count(3 * USES, 3 * u + 3))
                    for j in range(HG):
                        if x_ == CA:
                            last = nc.tensor.matmul(bank[DH * j:DH * (j + 1), :], ones[:], probs[:, T - 1, j, :],
                                                    start=True, stop=True)
                        else:
                            for i in range(T):
                                last = nc.tensor.matmul(bank[DH * i:DH * (i + 1), P * j:P * (j + 1)], ones[:],
                                                        probs[:, T - 1, j, P * i:P * (i + 1)], start=True, stop=True)
                    last.then_inc(denom_done, 1)
                elif kind == "back":
                    g = step[1]
                    bank = claim(("back_d", g))
                    written([("denom", CA, g)], ("back_d", g))
                    for t in range(T):
                        last = nc.tensor.transpose(bank[:, P * t:P * (t + 1)], den[:, P * t:P * (t + 1)], ident[:])
                    last.then_inc(back_d, 1)
                    bank = claim(("back_o", g))
                    pe.wait_ge(attn_out, at.count(USES, G + g + 1))
                    for t in range(T):
                        last = nc.tensor.transpose(bank[:, P * t:P * (t + 1)], attn_raw[:, g % 2, P * t:P * (t + 1)], ident[:])
                    last.then_inc(back_o, 1)
                elif kind == "out_proj":
                    t = step[1]
                    bank = claim(step)
                    pe.wait_ge(div_used, at.count(USES, G))
                    if t == 0:
                        need(pe, w_lo, 2)
                    n = 0
                    for k in range(KD):
                        for a, c in ((0, 0), (0, 1), (1, 0)):
                            last = nc.tensor.matmul(bank, actT[:, a, k, P * t:P * (t + 1)], wo[:, c, k, :],
                                                    start=n == 0, stop=n == 3 * KD - 1)
                            n += 1
                    last.then_inc(outproj_done, 1)
                elif kind == "gate_up":
                    _, hf, m = step
                    bank = claim(step)
                    if m == 0:
                        written([("norm", 3, 2 * hf + 1)], step)
                        need(pe, w_int, 2 * KD)
                    for half, wt in enumerate((wg, wu)):
                        for k in range(KD):
                            for a in (0, 1):
                                last = nc.tensor.matmul(bank[:, HALF * half:HALF * (half + 1)], wt[:, k, P * m:P * (m + 1)],
                                                        x3T[:, a, k, :], start=k == 0 and a == 0, stop=k == KD - 1 and a == 1)
                    last.then_inc(gu_filled, 1)
                elif kind == "down":
                    _, hf, t = step
                    bank = claim(step)
                    ma = mlp_at(hf, at)
                    pe.wait_ge(hid_lo, ma.count(2 * MH, MH * (hf + 1)))
                    if hf == 0 and t == 0:
                        need(pe, w_int, 3 * KD)
                    tt = t - 2 * hf
                    for m in range(MH):
                        for a in (0, 1):
                            last = nc.tensor.matmul(bank, hid[:, a, m, P * tt:P * (tt + 1)], wd[:, m, :],
                                                    start=m == 0 and a == 0, stop=m == MH - 1 and a == 1)
                    last.then_inc(down_done, 1)
            walk(pe, do)

        @block.scalar
        def _(act):
            for n, (raw, parts) in enumerate(((wv_raw, wv), (wo_raw, wo))):
                act.wait_ge(wraw_in[n], 16)
                nc.scalar.activation(parts[:, 0], raw, ACT.Copy, scale=SW).then_inc(w_hi, 1)

            def hidden_hi(hf, m, at, w):
                key = ("gate_up", hf, m)
                act.wait_ge(work_free[w.bank(key)], w.released(key, at))
                nc.scalar.activation(hid[:, 0, m, :], hraw[:, m % 2, :], ACT.Copy).then_inc(hid_hi, 1)

            def do(step, at, w):
                kind = step[0]
                if kind == "norm":
                    _, ln, t = step
                    la = ln_at(ln, t, at)
                    act.wait_ge(norm_t[ln], la.count(T, t + 1))
                    src = work[:, w.bank(step), :].rearrange("p (k s) -> p k s", k=KD)
                    if ln == 2 and t == 0:
                        act.wait_ge(*k_ready(CA, at))
                    if ln == 3:
                        dst = x3T[:, 0, :, P * (t % 2):P * (t % 2 + 1)]
                    else:
                        dst = (actT if ln == 1 else pqT)[:, 0, :, P * t:P * (t + 1)]
                    nc.scalar.activation(dst, src, ACT.Copy, scale=SX).then_inc(norm_hi[ln], 1)
                elif kind == "proj_t":
                    g = step[1]
                    act.wait_ge(projt_done, at.plus(1).count(G, g + 1))
                    nc.scalar.activation(pqT[:, 0, g, :], work[:, w.bank(step), :], ACT.Copy,
                                         scale=SP_).then_inc(projt_hi, 1)
                elif kind == "shift":
                    _, x_, g = step
                    u = G * x_ + g
                    need(act, shift_in, at.count(16 * USES, 16 * u))
                    act.wait_ge(shift_t, at.count(USES, u + 1))
                    nc.scalar.activation(shift_row[:], work[0:HG, w.bank(step), :], ACT.Copy,
                                         scale=1.0 / (SHIFT_SA, SHIFT_CA)[x_]).then_inc(work_free[w.bank(step)], 1)
                elif kind == "probs":
                    _, x_, g, kt = step
                    u = G * x_ + g
                    if kt < T - 1:
                        need(act, sums, at.count(3 * USES, 3 * (u - 1) + kt + 1))
                    else:
                        need(act, denom_done, at.count(USES, u))
                    for j in range(HG):
                        r = kt * HG + j
                        act.wait_ge(b_filled, at.count(USES * UNITS, u * UNITS + r + 1))
                        nc.scalar.activation(probs[:, kt, j, :], score_b[:, r % 3, :], ACT.Exp,
                                             scale=(1.0 / (SP_ * SP_ * DH ** 0.5), 1.0 / CA_SCORE)[x_]).then_inc(exp_done, 1)
                elif kind == "values" and step[3] == T - 1:
                    _, x_, g, kt = step
                    u = G * x_ + g
                    if (u - 2) % USES < G:
                        need(act, div_done, at.count(G, g - 1 if x_ == SA else G - 1 + g))
                    else:
                        need(act, back_o, at.count(G, g - 1 if x_ == CA else g - G + G - 1))
                    act.wait_ge(values_done, at.count(USES * T, T * (u + 1)))
                    nc.scalar.activation(attn_raw[:, g % 2, :], attn[:], ACT.Copy).then_inc(attn_out, 1)
                elif kind == "denom" and step[1] == CA:
                    g = step[2]
                    act.wait_ge(denom_done, at.count(USES, G + g + 1))
                    need(act, back_d, at.count(G, g))
                    nc.scalar.activation(den[:], work[:, w.bank(step), :], ACT.Copy).then_inc(work_free[w.bank(step)], 1)
                elif kind == "finish" and step[1] == SA:
                    g = step[2]
                    act.wait_ge(div_done, at.count(G, g + 1))
                    nc.scalar.activation(folded(0, g), attn_div[:].rearrange("p (j k b) -> p j k b", j=HG, k=KD),
                                         ACT.Copy).then_inc(div_hi, 1)
                elif kind == "keys":
                    g = step[1]
                    act.wait_ge(key_in, at.count(16 * G, 16 * (g + 1)))
                    if g == 0:
                        act.wait_ge(*q_ready(SA, at))
                        act.wait_ge(*k_ready(SA, at))
                    nc.scalar.activation(pqT[:, 0, g, :], keyT[:], ACT.Copy, scale=SP_).then_inc(key_hi, 1)
                elif kind == "gate_up":
                    _, hf, m = step
                    ma = mlp_at(hf, at)
                    act.wait_ge(gu_filled, ma.count(2 * MH, MH * hf + m + 1))
                    nc.scalar.activation(th[:, m % 2, :], work[:, w.bank(step), 0:HALF], ACT.Tanh,
                                         scale=0.5 * DEQ / SX).then_inc(tanh_done, 1)
                    if m:
                        hidden_hi(hf, m - 1, at, w)
                elif kind == "hidden_end":
                    hidden_hi(step[1], MH - 1, at, w)
                elif kind == "weights":
                    c = step[1]
                    act.wait_ge(wraw_in[c % 2], 16 + 16 * (c // 2 + 1))
                    src, k = divmod(c, KD)
                    dst = (wg[:, k, :], wu[:, k, :], wd[:, 3 * k:3 * (k + 1), :].rearrange("p m n -> p (m n)"))[src]
                    nc.scalar.activation(dst, w_raw[:, c % 2], ACT.Copy).then_inc(w_int, 1)
            walk(act, do)

        @block.vector
        def _(dve):
            for n, (raw, parts) in enumerate(((wv_raw, wv), (wo_raw, wo))):
                dve.wait_ge(w_hi, n + 1)
                nc.vector.scalar_tensor_tensor(parts[:, 1].rearrange("p k e -> p (k e)"), raw.rearrange("p k e -> p (k e)"),
                                               SW, parts[:, 0].rearrange("p k e -> p (k e)"),
                                               ALU.mult, ALU.subtract).then_inc(w_lo, 1)
                if n == 0:
                    dve.wait_ge(consts_in, 16 * 6)
                    nc.vector.tensor_copy(len8f, len8i).then_inc(table_step, 1)
                    dve.wait_ge(table_step, 1)
                    nc.vector.tensor_scalar(gate8, len8f, 0.0, None, ALU.is_gt).then_inc(table_step, 1)
                    dve.wait_ge(table_step, 2)
                    nc.vector.tensor_scalar(inv8, pos8, len8f, gate8, ALU.is_ge, ALU.mult).then_inc(table_step, 1)
                    dve.wait_ge(table_step, 3)
                    nc.vector.tensor_scalar(rows8[:, 2], inv8, -65504.0, None, ALU.mult).then_inc(table_step, 1)
                    nc.vector.tensor_scalar(bias8, bias8, gate8, SP_, ALU.mult, ALU.mult).then_inc(table_step, 1)
                    dve.wait_ge(table_step, 5)
                    nc.vector.tensor_copy(rows8[:, 0], bias8).then_inc(table_step, 1)
                    dve.wait_ge(table_step, 6)
                    nc.vector.tensor_tensor(rows8[:, 1], bias8, rows8[:, 0], ALU.subtract).then_inc(table_step, 1)
                    nc.vector.tensor_copy(gate[:], lens_i[:]).then_inc(table_step, 1)
                    dve.wait_ge(table_step, 8)
                    nc.vector.tensor_scalar(gate[:], gate[:], 0.0, DH ** -0.5, ALU.is_gt, ALU.mult).then_inc(table_step, 1)

            def do(step, at, w):
                kind = step[0]
                if kind == "stats":
                    _, ln, t = step
                    la = ln_at(ln, t, at)
                    if ln == 1:
                        dve.wait_ge(xin_in, la.count(16 * KD, 16 * KD))
                        src = xin
                    elif ln == 2:
                        key = ("out_proj", t)
                        dve.wait_ge(work_free[w.bank(key)], w.released(key, at))
                        src = res1
                    else:
                        dve.wait_ge(moved, la.count(1, 1))
                        src = res2
                    nc.vector.bn_stats(bst[:, ln - 1, t, :], src[:, t, :]).then_inc(stat[ln], 1)
                elif kind == "rstd":
                    _, ln, tiles = step
                    la = ln_at(ln, tiles[-1], at)
                    dve.wait_ge(stat[ln], la.count(T, tiles[-1] + 1))
                    nc.vector.memset(carrier[:], 0.0)
                    for t in tiles:
                        nc.vector.bn_aggr(mv[:, ln - 1, t, :], bst[:, ln - 1, t, :]).then_inc(meanvar[ln], 1)
                elif kind == "norm":
                    _, ln, t = step
                    la = ln_at(ln, t, at)
                    ops = {1: 2, 2: 3, 3: 4}[ln]
                    dve.wait_ge(rstd[ln], la.count(ops, ops if ln < 3 or t >= 2 else 2))
                    if t >= 2:
                        dve.wait_ge(norm_t[ln], la.count(T, t - 1))
                    nc.vector.tensor_scalar(xn[:, t % 2 + 2 * (ln == 3), :], (xin, res1, res2)[ln - 1][:, t, :],
                                            mv[:, ln - 1, t, 0:1], rs[:, ln - 1, t:t + 1],
                                            ALU.subtract, ALU.mult).then_inc(normed[ln], 1)
                elif kind == "norm_lo":
                    _, ln, t = step
                    la = ln_at(ln, t, at)
                    key = ("norm", ln, t)
                    dve.wait_ge(norm_hi[ln], la.count(T, t + 1))
                    src = work[:, w.bank(key), :].rearrange("p (k s) -> p k s", k=KD)
                    buf, col = (x3T, t % 2) if ln == 3 else (actT if ln == 1 else pqT, t)
                    nc.vector.scalar_tensor_tensor(buf[:, 1, :, P * col:P * (col + 1)], src, SX,
                                                   buf[:, 0, :, P * col:P * (col + 1)],
                                                   ALU.mult, ALU.subtract).then_inc(work_free[w.bank(key)], 1)
                elif kind == "proj":
                    t = step[1]
                    dve.wait_ge(proj_done, at.plus(1).count(T, t + 1))
                    nc.vector.scalar_tensor_tensor(v_self[:, t, :], work[:, w.bank(step), :], 1.0 / (SX * SW), bvb[:],
                                                   ALU.mult, ALU.add).then_inc(work_free[w.bank(step)], 1)
                elif kind == "proj_lo":
                    g = step[1]
                    key = ("proj_t", g)
                    dve.wait_ge(projt_hi, at.plus(1).count(G, g + 1))
                    nc.vector.scalar_tensor_tensor(pqT[:, 1, g, :], work[:, w.bank(key), :], SP_, pqT[:, 0, g, :],
                                                   ALU.mult, ALU.subtract).then_inc(work_free[w.bank(key)], 1)
                elif kind == "maxima":
                    _, x_, g, j = step
                    u = G * x_ + g
                    if j == 0:
                        need(dve, shift_t, at.count(USES, u - 1))
                    for t in range(T):
                        n = u * UNITS + j * T + t
                        dve.wait_ge(a_filled, at.count(USES * UNITS, n + 1))
                        nc.vector.tensor_reduce(negmax[:, g % 2, t, j:j + 1], score_a[:, n % 2, :], AX_X, ALU.max,
                                                negate=True).then_inc(max_done, 1)
                elif kind == "finish" and step[1] == SA:
                    g = step[2]
                    key = ("denom", SA, g)
                    dve.wait_ge(denom_done, at.count(USES, g + 1))
                    nc.vector.reciprocal(den[:], work[:, w.bank(key), :]).then_inc(work_free[w.bank(key)], 1)
                    dve.wait_ge(work_free[w.bank(key)], w.released(key, at))
                    dve.wait_ge(attn_out, at.count(USES, g + 1))
                    need(dve, div_used, at.count(USES, g))
                    nc.vector.scalar_tensor_tensor(attn_div[:], attn_raw[:, g % 2, :], SP_, den[:],
                                                   ALU.mult, ALU.mult).then_inc(div_done, 1)
                elif kind == "back":
                    g = step[1]
                    kd, ko = ("back_d", g), ("back_o", g)
                    dve.wait_ge(back_d, at.count(G, g + 1))
                    nc.vector.reciprocal(rcol[:], work[:, w.bank(kd), :].rearrange("p (n i) -> p n i", i=DH)[:, :, 0]
                                         ).then_inc(work_free[w.bank(kd)], 1)
                    dve.wait_ge(back_o, at.count(G, g + 1))
                    dve.wait_ge(work_free[w.bank(kd)], w.released(kd, at))
                    need(dve, div_used, at.count(USES, G + g))
                    nc.vector.tensor_tensor(attn_div[:].rearrange("p (n i) -> p n i", i=DH),
                                            work[:, w.bank(ko), :].rearrange("p (n i) -> p n i", i=DH),
                                            rcol[:].unsqueeze(2).broadcast_to([P, T * HG, DH]),
                                            ALU.mult).then_inc(work_free[w.bank(ko)], 1)
                elif kind == "out_proj":
                    t = step[1]
                    dve.wait_ge(outproj_done, at.count(T, t + 1))
                    if t == 0:
                        dve.wait_ge(bo_added, at.count(1, 1))
                    nc.vector.scalar_tensor_tensor(res1[:, t, :], work[:, w.bank(step), :], 1.0 / (SP_ * SW), res1[:, t, :],
                                                   ALU.mult, ALU.add).then_inc(work_free[w.bank(step)], 1)
                elif kind == "keys":
                    g = step[1]
                    dve.wait_ge(key_hi, at.count(G, g + 1))
                    nc.vector.scalar_tensor_tensor(pqT[:, 1, g, :], keyT[:], SP_, pqT[:, 0, g, :],
                                                   ALU.mult, ALU.subtract).then_inc(key_lo, 1)
                elif kind == "residual":
                    dve.wait_ge(div_used, at.count(USES, USES))
                    need(dve, stored, at.count(16 * T, 0))
                    nc.vector.tensor_copy(res2[:], res1[:]).then_inc(moved, 1)
                elif kind == "gate_up":
                    _, hf, m = step
                    ma = mlp_at(hf, at)
                    n = MH * hf + m
                    bank = work[:, w.bank(step), :]
                    dve.wait_ge(tanh_done, ma.count(2 * MH, n + 1))
                    nc.vector.scalar_tensor_tensor(th[:, m % 2, :], th[:, m % 2, :], 1.0, bank[:, 0:HALF],
                                                   ALU.add, ALU.mult).then_inc(silu_done, 1)
                    dve.wait_ge(silu_done, ma.count(2 * MH, n + 1))
                    need(dve, hid_lo, ma.count(2 * MH, n - 1))
                    nc.vector.scalar_tensor_tensor(hraw[:, m % 2, :], th[:, m % 2, :], 0.5 * SHID * (DEQ / SX) ** 2,
                                                   bank[:, HALF:2 * HALF], ALU.mult, ALU.mult
                                                   ).then_inc(work_free[w.bank(step)], 1)
                elif kind == "down":
                    _, hf, t = step
                    dve.wait_ge(down_done, mlp_at(hf, at).count(T, t + 1))
                    nc.vector.scalar_tensor_tensor(res2[:, t, :], work[:, w.bank(step), :], DEQ / SHID, res2[:, t, :],
                                                   ALU.mult, ALU.add).then_inc(work_free[w.bank(step)], 1)
            walk(dve, do)

        @block.gpsimd
        def _(pool):
            nc.gpsimd.memset(ident[:], 0.0).then_inc(consts_made, 1)
            pool.wait_ge(consts_made, 1)
            nc.gpsimd.affine_select(out=ident[:], in_=ident[:], compare_op=ALU.not_equal, fill=1.0, base=0,
                                    pattern=[[-1, P]], channel_multiplier=1).then_inc(consts_made, 1)
            nc.gpsimd.memset(ones[:], 1.0).then_inc(consts_made, 1)
            nc.gpsimd.memset(powers[:, 0, :], EPS).then_inc(consts_made, 1)
            nc.gpsimd.memset(powers[:, 1, :], -0.5).then_inc(consts_made, 1)
            nc.gpsimd.memset(rcol[:], 1.0).then_inc(consts_made, 1)
            pool.wait_ge(consts_made, 6)

            def hidden_lo(hf, m, at):
                pool.wait_ge(hid_hi, mlp_at(hf, at).count(2 * MH, MH * hf + m + 1))
                nc.gpsimd.tensor_tensor(hid[:, 1, m, :], hraw[:, m % 2, :], hid[:, 0, m, :],
                                        ALU.subtract).then_inc(hid_lo, 1)

            def do(step, at, w):
                kind = step[0]
                if kind == "rstd":
                    _, ln, tiles = step
                    a, b = tiles[0], tiles[-1] + 1
                    la = ln_at(ln, a, at)
                    ops = {1: 2, 2: 3, 3: 4}[ln]
                    n = 2 if ln == 3 and a else 0
                    r = rs[:, ln - 1, a:b]
                    pool.wait_ge(meanvar[ln], la.count(T, b))
                    nc.gpsimd.tensor_tensor(r, mv[:, ln - 1, a:b, 1], powers[:, 0, a:b], ALU.add).then_inc(rstd[ln], 1)
                    pool.wait_ge(rstd[ln], la.count(ops, n + 1))
                    nc.gpsimd.tensor_tensor(r, r, powers[:, 1, a:b], ALU.pow).then_inc(rstd[ln], 1)
                    if ln == 2:
                        pool.wait_ge(rstd[ln], la.count(ops, n + 2))
                        if at.reg is None and at.off == 0:
                            pool.wait_ge(table_step, 9)
                        nc.gpsimd.tensor_tensor(r, r, gate[:, bass.ds(at.index(), 1)].broadcast_to([P, T]),
                                                ALU.mult).then_inc(rstd[ln], 1)
                elif kind == "add_bo":
                    la = at.plus(1)
                    pool.wait_ge(x_in, la.count(16, 16))
                    if at.reg is None and at.off == -1:
                        pool.wait_ge(consts_in, 16 * 6)
                    nc.gpsimd.tensor_tensor(res1[:], res1[:], bob[:].unsqueeze(1).broadcast_to([P, T, D]),
                                            ALU.add).then_inc(bo_added, 1)
                elif kind == "values" and step[3]:
                    _, x_, g, kt = step
                    u = G * x_ + g
                    pool.wait_ge(values_done, at.count(USES * T, T * u + kt + 1))
                    if kt > 1:
                        pool.wait_ge(sums, at.count(3 * USES, 3 * u + kt - 1))
                    nc.gpsimd.tensor_tensor(probs[:, kt], probs[:, kt - 1], probs[:, kt], ALU.add).then_inc(sums, 1)
                elif kind == "finish" and step[1] == SA:
                    g = step[2]
                    pool.wait_ge(div_hi, at.count(G, g + 1))
                    nc.gpsimd.tensor_tensor(folded(1, g), attn_div[:].rearrange("p (j k b) -> p j k b", j=HG, k=KD),
                                            folded(0, g),
                                            ALU.subtract).then_inc(div_used, 1)
                elif kind == "back":
                    g = step[1]
                    key = ("back_o", g)
                    pool.wait_ge(work_free[w.bank(key)], w.released(key, at))
                    dst = res1[:, :, P * g:P * (g + 1)]
                    nc.gpsimd.tensor_tensor(dst, dst, attn_div[:].rearrange("p (t e) -> p t e", t=T),
                                            ALU.add).then_inc(div_used, 1)
                elif kind == "gate_up" and step[2]:
                    hidden_lo(step[1], step[2] - 1, at)
                elif kind == "hidden_end":
                    hidden_lo(step[1], MH - 1, at)
            walk(pool, do)


def kernel(x, ctx_2048, itok_Bx1_68_817, L0_attn_Wv, L0_attn_bv, L0_attn_Wo, L0_attn_bo, L0_xattn_b,
           L0_ffn_w_gate, L0_ffn_w_up, L0_ffn_w_down):
    import concourse.bacc as bacc
    from concourse.bass_utils import run_bass_kernel_spmd

    ctx = np.ascontiguousarray(ctx_2048)
    arrays = {
        "x": np.ascontiguousarray(x),
        "ctx": ctx,
        "ctx_kT": np.ascontiguousarray(ctx[:, :, :D].transpose(0, 2, 1)),
        "lens": np.ascontiguousarray(itok_Bx1_68_817),
        "wvT": np.ascontiguousarray(np.asarray(L0_attn_Wv).T),
        "bv": np.ascontiguousarray(L0_attn_bv),
        "woT": np.ascontiguousarray(np.asarray(L0_attn_Wo).T),
        "bo": np.ascontiguousarray(L0_attn_bo),
        "key_bias": np.ascontiguousarray(L0_xattn_b),
        "wgT": np.ascontiguousarray(np.asarray(L0_ffn_w_gate).T),
        "wuT": np.ascontiguousarray(np.asarray(L0_ffn_w_up).T),
        "wdT": np.ascontiguousarray(np.asarray(L0_ffn_w_down).T),
        "positions": np.arange(S, dtype=np.float32)[None, :],
        "row_consts": np.repeat(np.array([[1024.0], [1024.0], [32768.0], [16384.0]], np.float16), H * S, axis=1),
    }
    nc = bacc.Bacc("TRN2", target_bir_lowering=False, num_devices=1,
                   dynamic_dma_scratch_size=1024)
    args = [nc.dram_tensor(f"in_{n}", a.shape, mybir.dt.from_np(a.dtype), kind="ExternalInput").ap()
            for n, a in arrays.items()]
    out = nc.dram_tensor("out", (B, S, D), F32, kind="ExternalOutput").ap()
    build(nc, *args, out)
    r = run_bass_kernel_spmd(nc, [{f"in_{n}": a for n, a in arrays.items()}], core_ids=[0])
    return r.results[0]["out"]
```

```python
from contextlib import ExitStack

import numpy as np

import concourse.bass as bass
from concourse import mybir

F32 = mybir.dt.float32
F16 = mybir.dt.float16
I32 = mybir.dt.int32
ALU = mybir.AluOpType
ACT = mybir.ActivationFunctionType
AX_X = mybir.AxisListType.X

P = 128
B, S, D, H = 8, 512, 512, 16
DH = D // H
T = S // P
KD = D // P
G = 4
HG = H // G
HID = 1536
MH = HID // P
HALF = S // 2
EPS = 1e-5

SX = 1024.0
SW = 64.0
SP_ = 16.0
SHID = 0.125
DEQ = 1.0 / 127.0
CA_SCORE = SX * SP_
SHIFT_SA, SHIFT_CA = 1024.0, 16384.0
SA, CA = 0, 1
K_MAX = {SA: 3 * DH, CA: 3 * DH + 3}
SHIFT_ROW = {SA: 3 * DH, CA: 3 * DH + 3}
USES = 2 * G
UNITS = T * HG


class At:

    def __init__(self, reg, off=0):
        self.reg, self.off = reg, off

    def plus(self, n):
        return At(self.reg, self.off + n)

    def count(self, per_batch, within):
        fixed = self.off * per_batch + within
        return fixed if self.reg is None else self.reg * per_batch + fixed

    def index(self):
        return self.off if self.reg is None else self.reg + self.off


class Work:

    def __init__(self, steps, before, first):
        self.number, self.before, self.first = {}, before, first
        for step in steps:
            for key in work_units(step):
                self.number[key] = len(self.number)
        self.units = len(self.number)

    def bank(self, key):
        return self.number[key] % 2

    def released(self, key, at):
        n = self.before + self.number[key]
        base = n // 2 + 1
        return at.plus(-self.first).count(self.units // 2, base)

    def free(self, key, at):
        n = self.before + self.number[key]
        return at.plus(-self.first).count(self.units // 2, n // 2)


def work_units(step):
    kind = step[0]
    if kind == "denom":
        return [step[:3]] if step[3][0] == 0 else []
    if kind == "down":
        return [step[:3]] if step[3][0] == 0 else []
    if kind in ("proj", "out_proj", "shift", "back_d", "back_o", "gate_up"):
        return [step]
    return []


def norm_piece(ln, t):
    return [("norm", ln, t), ("norm_lo", ln, t)]


def stats_pieces(ln, tiles):
    return [[("stats", ln, t)] for t in tiles] + [[("rstd", ln, tiles)]]


def project_pieces():
    return [[("proj", t), ("proj_add", t)] for t in range(T)] + [[("proj_t", t), ("proj_lo", t)] for t in range(T)]


def out_piece(t):
    return [("out_proj", t), ("out_add", t)]


def gate_up_pieces(hf):
    return [[("gate_up", hf, m), ("silu", hf, m)] + ([("hidden_end", hf)] if m == MH - 1 else []) for m in range(MH)]


def down_piece(hf, t):
    return [("down", hf, t, tuple(range(MH))), ("down_add", hf, t)]


def down_spread(hf, t):
    return [("down", hf, t, (m, m + 1)) for m in range(0, MH, 2)] + [("down_add", hf, t)]


def pipeline(pieces):
    out, late = [], []
    for p in pieces:
        if not p:
            out += late
            late = []
        elif len(p) == 1:
            out += p
        else:
            out += p[:1] + late
            late = p[1:]
    return out + late


def attention_steps(x, head, late, end):
    out, divides = [], {}
    for n in range(-LEAD, G * UNITS + LAG + 1):
        a = n + LEAD
        if a < G * UNITS:
            out.append(("maxima", x, a))
        g, r = divmod(a - UNITS, UNITS)
        if r == 1 and 0 <= g < G:
            out.append(("shift", x, g))
        if r == 2 and 0 <= g < G:
            out.append(("shift_row", x, g))
        if 0 <= n < G * UNITS:
            out.append(("probs", x, n))
        if n < 0:
            out += head[len(head) * a // LEAD:len(head) * (a + 1) // LEAD]
        g, r = divmod(n - LAG, UNITS)
        if r % HG == HG - 1 and 0 <= g < G:
            out.append(("values", x, g, r // HG))
        if r == 0 and 1 <= g <= G:
            out.append(("evacuate", x, g - 1))
        g, r = n // UNITS - 1, n % UNITS
        if 0 <= g < G - 1:
            if r == 3:
                out.append(("denom", x, g, (0,)))
            elif r == DENOM2:
                out.append(("denom", x, g, (1,)))
                if x == SA:
                    divides = {n + 1 + q * (2 if g == 0 else 1): ("divide", g, (q,)) for q in range(T)}
            elif x == CA and r == DENOM2 + 1:
                out.append(("den_copy", g))
            elif x == CA and r > DENOM2 + 2:
                out += ([("back_d", g)], [("back_r", g), ("back_o", g)], [("back_add", g)])[r - DENOM2 - 3]
        if n in divides:
            out.append(divides.pop(n))
        if x == SA and r == 6 and 1 <= g <= G - 2:
            out.append(("fold", g - 1))
        if x == SA and r == 12 and -1 <= g < G - 1:
            out.append(("keys", g + 1))
        if x == SA and n == 3 * UNITS + 1:
            out.append(("stack_keys", (0, 1, 2)))
        out += late.get(n, [])
    return out + end


LEAD = 25
LAG = 2
DENOM2 = 10


def batch_steps(first, last):
    beside = [[("weights", c), ("to_half", c)] for c in range(MH)] if first else gate_up_pieces(1)
    late = {49: [("out_proj", 0)], 50: [("out_add", 0)], 52: [("stats", 2, 0)], 53: [("rstd", 2, [0])],
            62: [("scale", 2, 0)], 63: [("norm", 2, 0)], 64: [("out_proj", 1), ("norm_lo", 2, 0)], 65: [("out_add", 1)]}
    b = beside
    end = pipeline(
        [[("fold", 2)]] + stats_pieces(2, [1]) + b[:3] + [[("denom", SA, 3, (0, 1)), ("divide", 3, (0, 1, 2, 3))]]
        + [[("scale", 2, 1)], out_piece(2), norm_piece(2, 1)] + stats_pieces(2, [2]) + b[3:4] + [[("fold", 3)]] + b[4:5]
        + [[("scale", 2, 2)]] + b[5:6] + [norm_piece(2, 2)]
        + b[6:7] + [out_piece(3)] + b[7:8] + stats_pieces(2, [3]) + b[8:9] + [[("scale", 2, 3)]] + b[9:10] + [norm_piece(2, 3)]
        + [[("queries",)], [("stack_keys", (3,))]] + b[10:] + ([] if first else [down_piece(1, 2)]))
    head = [] if last else [("load_ordered",)]
    downs = [] if first else down_spread(0, 0) + down_spread(0, 1)
    out = head + downs[:2] + attention_steps(SA, downs[2:], late, end)
    late = {} if last else {
        40: [("stats", 1, 0)], 41: [("stats", 1, 1)], 44: [("stats", 1, 2)], 45: [("stats", 1, 3)],
        46: [("rstd", 1, [0, 1, 2, 3])], 48: [("scale", 1, 0)], 49: [("norm", 1, 0), ("scale", 1, 1)],
        50: [("norm_lo", 1, 0)], 51: [("norm", 1, 1)], 52: [("scale", 1, 2)], 53: [("norm_lo", 1, 1)],
        55: [("norm", 1, 2)], 56: [("scale", 1, 3)], 57: [("norm_lo", 1, 2)], 58: [("norm", 1, 3)],
        60: [("norm_lo", 1, 3)]}
    pr = [] if last else project_pieces()
    load = [] if last else [[("stack_proj",)], [("load_x",)], [("load_v",)]]
    end = pipeline(
        pr[:2] + [[("denom", CA, 3, (0, 1)), ("den_copy", 3)]] + pr[4:5] + [[("back_d", 3), ("back_r", 3)]]
        + pr[5:6] + [[("back_o", 3), ("back_add", 3)]] + (pr[2:4] or [[]]) + stats_pieces(3, [0, 1]) + pr[6:7]
        + [[("scale", 3, 0)], [("scale", 3, 1)]] + pr[7:8] + load
        + [norm_piece(3, 0), norm_piece(3, 1)] + stats_pieces(3, [2, 3]) + gate_up_pieces(0)
        + [[("scale", 3, 2)], [("scale", 3, 3)], norm_piece(3, 2), norm_piece(3, 3)] + ([] if last else [[("add_bo",)]]))
    return out + attention_steps(CA, [] if first else down_spread(1, 3), late, end)


def start_steps():
    pr = project_pieces()
    norms = sum([[[("scale", 1, t)], norm_piece(1, t)] for t in range(T)], [])
    return pipeline(stats_pieces(1, [0, 1, 2, 3]) + norms + [[("add_bo",)]]
                    + pr[:2] + [pr[4], pr[2], pr[5], pr[3], pr[6], pr[7]] + [[("stack_proj",)]])


def tail_steps():
    return pipeline([down_piece(0, 0), down_piece(0, 1)] + gate_up_pieces(1) + [down_piece(1, 2), down_piece(1, 3)])


def build(nc, x, ctx, ctx_kT, lens, wvT, bv, woT, bo, key_bias, wgT, wuT, wdT, positions, row_consts, out):
    plans = {}
    order = []
    before = 0
    for name, steps, first in (
            ("start", start_steps(), -1),
            ("batch0", batch_steps(True, False), 0),
            ("loop", batch_steps(False, False), 1),
            ("last", batch_steps(False, True), B - 1),
            ("tail", tail_steps(), B)):
        w = Work(steps, before, first)
        plans[name] = (steps, w)
        order.append(name)
        assert w.units % 2 == 0
        before += w.units * (B - 2 if name == "loop" else 1)

    with ExitStack() as es:
        def sb(name, shape, dt):
            return es.enter_context(nc.sbuf_tensor(name, shape, dt))

        def ps(name, shape):
            return es.enter_context(nc.psum_tensor(name, shape, F32))

        def sem(name):
            return es.enter_context(nc.semaphore(name))

        wv = sb("wv", [P, 2, KD, D], F16)
        wo = sb("wo", [P, 2, KD, D], F16)
        wg = sb("wg", [P, KD, HID], F16)
        wu = sb("wu", [P, KD, HID], F16)
        wd = sb("wd", [P, MH, D], F16)
        probs = sb("probs", [P, T, HG, S], F32)
        q_stack = sb("q_stack", [P, G, HG, S], F16)
        k_stack = sb("k_stack", [P, G, HG, S], F16)
        xin = sb("xin", [P, T, D], F32)
        res1 = sb("res1", [P, T, D], F32)
        res2 = sb("res2", [P, T, D], F32)
        xn = sb("xn", [P, 4, D], F32)
        actT = sb("actT", [P, 2, KD, S], F16)
        x3T = sb("x3T", [P, 2, KD, HALF], F16)
        hid = sb("hid", [P, 2, MH, HALF], F16)
        v_self = sb("v_self", [P, T, D], F32)
        v_ctx = sb("v_ctx", [P, T, D], F32)
        pqT = sb("pqT", [P, 2, KD, S], F16)
        keyT = sb("keyT", [P, S], F32)
        bvb = sb("bvb", [P, D], F32)
        bob = sb("bob", [P, D], F32)
        attn_raw = sb("attn_raw", [P, 2, S], F32)
        den = sb("den", [P, S], F32)
        attn_div = sb("attn_div", [P, S], F32)
        th = sb("th", [P, 2, HALF], F32)
        hraw = sb("hraw", [P, 2, HALF], F32)
        shift_row = sb("shift_row", [HG, S], F16)
        ident = sb("ident", [P, P], F32)
        ones = sb("ones", [P, DH], F32)
        negmax = sb("negmax", [P, 2, T, HG], F32)
        rcol = sb("rcol", [P, T * HG], F32)
        carrier = sb("carrier", [P, 1], F32)
        carrier_pool = sb("carrier_pool", [P, 1], F32)
        bst = sb("bst", [P, 3, T, 6], F32)
        mv = sb("mv", [P, 3, T, 2], F32)
        rs = sb("rs", [P, 3, T], F32)
        powers = sb("powers", [P, 2, T], F32)
        gate = sb("gate", [P, B], F32)
        lens_i = sb("lens_i", [P, B], I32)
        wv_raw = probs[:, 0]
        wo_raw = probs[:, 1]
        w_raw = hid[:].rearrange("p a m s -> p (a m s)").bitcast(I32).rearrange("p (c n) -> p c n", c=2)
        pos8 = probs[0:B, 2, 0]
        bias8 = probs[0:B, 2, 1]
        inv8 = probs[0:B, 2, 2]
        len8f = probs[0:B, 3, 0, 0:1]
        gate8 = probs[0:B, 3, 0, 1:2]
        len8i = probs[0:B, 3, 1, 0:1].bitcast(I32)
        rows8 = probs[0:B, 3, 2:4].rearrange("p a s -> p (a s)").bitcast(F16).rearrange(
            "p (r s) -> p r s", s=S)[:, 0:3]

        score_b = ps("score_b", [P, 3, S])
        score_a = ps("score_a", [P, 2, S])
        attn = ps("attn", [P, S])
        work = ps("work", [P, 2, S])

        key_rows = nc.dram_tensor("key_rows", [B, 3, S], F16, kind="Internal").ap()

        x_in = sem("x_in")
        xin_in = sem("xin_in")
        v_in = sem("v_in")
        key_in = sem("key_in")
        q_stacked = sem("q_stacked")
        k_stacked = sem("k_stacked")
        last_stacked = sem("last_stacked")
        shift_in = sem("shift_in")
        stored = sem("stored")
        consts_in = sem("consts_in")
        wraw_in = [sem("wraw_in0"), sem("wraw_in1")]
        rows_out = sem("rows_out")
        row99_in = sem("row99_in")
        consts_made = sem("consts_made")
        table_step = sem("table_step")
        w_hi = sem("w_hi")
        w_lo = sem("w_lo")
        w_int = sem("w_int")
        work_free = [sem("work_free0"), sem("work_free1")]
        stat = {ln: sem(f"stat{ln}") for ln in (1, 2, 3)}
        meanvar = {ln: sem(f"meanvar{ln}") for ln in (1, 2, 3)}
        rstd = {ln: sem(f"rstd{ln}") for ln in (1, 2, 3)}
        normed = {ln: sem(f"normed{ln}") for ln in (1, 2, 3)}
        norm_t = {ln: sem(f"norm_t{ln}") for ln in (1, 2, 3)}
        norm_hi = {ln: sem(f"norm_hi{ln}") for ln in (1, 2, 3)}
        bo_added = sem("bo_added")
        proj_done = sem("proj_done")
        v_made = sem("v_made")
        projt_done = sem("projt_done")
        projt_hi = sem("projt_hi")
        a_filled = sem("a_filled")
        max_done = sem("max_done")
        shift_t = sem("shift_t")
        b_filled = sem("b_filled")
        exp_done = sem("exp_done")
        values_done = sem("values_done")
        attn_out = sem("attn_out")
        sums = sem("sums")
        denom_done = sem("denom_done")
        div_done = sem("div_done")
        div_hi = sem("div_hi")
        div_used = sem("div_used")
        outproj_done = sem("outproj_done")
        key_hi = sem("key_hi")
        key_lo = sem("key_lo")
        back_d = sem("back_d")
        back_o = sem("back_o")
        gu_filled = sem("gu_filled")
        tanh_done = sem("tanh_done")
        silu_done = sem("silu_done")
        hid_hi = sem("hid_hi")
        hid_lo = sem("hid_lo")
        down_done = sem("down_done")
        side_free = sem("side_free")

        Q_PARTS = (0, 0, 1)
        K_PARTS = (0, 1, 0)
        BLOCKS = 16 * 3 * HG
        K_BLOCKS = 2 * BLOCKS + 16 * 4

        def q_ready(x_, at):
            return q_stacked, at.count(2 * BLOCKS + 16, BLOCKS if x_ == SA else 2 * BLOCKS + 16)

        def k_ready(x_, at):
            return k_stacked, at.count(K_BLOCKS, BLOCKS + 16 if x_ == SA else K_BLOCKS)

        def need(eng, s, value):
            if not isinstance(value, int) or value > 0:
                eng.wait_ge(s, value)

        def walk(eng, do):
            for name in order:
                steps, w = plans[name]
                if name == "loop":
                    with eng.Fori(1, B - 1) as b:
                        for step in steps:
                            do(step, At(b), w)
                else:
                    for step in steps:
                        do(step, At(None, w.first), w)

        def gu_at(hf, at):
            return at if hf == 0 else at.plus(-1)

        def ln_at(ln, at):
            return at.plus(1) if ln == 1 else at

        def side(kind, t, at):
            if at.reg is None and at.off < 0:
                return T * ("norm1", "v").index(kind) + t
            kinds = ("norm2", "norm3") if at.reg is None and at.off == B - 1 else ("norm2", "norm1", "v", "norm3")
            return at.count(4 * T, 2 * T + T * kinds.index(kind) + t)

        def side_before(x_, at):
            return at.count(4 * T, 2 * T + T * x_)

        def rstd_ops(ln, tiles):
            ops = 3 if ln == 2 else 2
            per, n = {1: (2, 1), 2: (12, tiles[-1] + 1), 3: (4, tiles[-1] // 2 + 1)}[ln]
            return per, ops * n

        def folded(part, g):
            return actT[:, part, :, P * g:P * (g + 1)].rearrange("p k (j b) -> p j k b", j=HG)

        block = es.enter_context(nc.Block())

        @block.sync
        def _(sp):
            def load_ordered(xb):
                rows = xb.rearrange("(b k j) d -> k b j d", k=KD, j=T)
                for k in range(KD):
                    sp.dma_start(xin[DH * k:DH * (k + 1)], rows[k]).then_inc(xin_in, 16)

            load_ordered(x[0])
            sp.dma_start(res1[:], x[0].rearrange("(t p) d -> p t d", p=P)).then_inc(x_in, 16)
            sp.dma_start(wv_raw, wvT.rearrange("(k p) e -> p k e", p=P)).then_inc(wraw_in[0], 16)
            sp.dma_start(bvb[:], bv.rearrange("(o d) -> o d", o=1).broadcast_to([P, D])).then_inc(consts_in, 16)
            sp.dma_start(bob[:], bo.rearrange("(o d) -> o d", o=1).broadcast_to([P, D])).then_inc(consts_in, 16)
            sp.dma_start(pos8, positions.broadcast_to([B, S])).then_inc(consts_in, 16)
            sp.dma_start(bias8, key_bias.rearrange("(o d) -> o d", o=1).broadcast_to([B, S])).then_inc(consts_in, 16)
            sp.dma_start(len8i, lens).then_inc(consts_in, 16)
            sp.dma_start(lens_i[:], lens.rearrange("b o -> o b").broadcast_to([P, B])).then_inc(consts_in, 16)
            sp.dma_start(wo_raw, woT.rearrange("(k p) e -> p k e", p=P)).then_inc(wraw_in[1], 16)
            sp.dma_start(k_stack[99:100], row_consts[3:4].rearrange("r (g j s) -> r g j s", g=G, j=HG)
                         ).then_inc(row99_in, 16)
            sp.dma_start(v_ctx[:], ctx[0, :, D:2 * D].rearrange("(t p) d -> p t d", p=P)).then_inc(v_in, 16)
            sp.wait_ge(table_step, 9)
            sp.dma_start(key_rows, rows8).then_inc(rows_out, 16)
            sp.wait_ge(rows_out, 16)

            def load_keys(at, g):
                sp.dma_start(keyT[:], ctx_kT[bass.ds(at.index(), 1), P * g:P * (g + 1), :].rearrange(
                    "o e s -> (o e) s")).then_inc(key_in, 16)

            load_keys(At(None, 0), 0)

            def fill_stack(stack, src, parts, done, groups=range(G)):
                a, b = groups[0], groups[-1] + 1
                for j in range(HG):
                    for r, part in enumerate(parts):
                        sp.dma_start(stack[DH * r:DH * (r + 1), a:b, j, :],
                                     src[DH * j:DH * (j + 1), part, a:b]).then_inc(done, 16)

            def do(step, at, w):
                kind = step[0]
                if kind == "load_x" and not (at.reg is None and at.off == -1):
                    sp.wait_ge(div_used, at.count(USES, USES))
                    sp.dma_start(res1[:], x[bass.ds(at.plus(1).index(), 1)].rearrange(
                        "o (t p) d -> p (o t) d", p=P)).then_inc(x_in, 16)
                elif kind == "load_ordered" and not (at.reg is None and at.off == -1):
                    sp.wait_ge(normed[1], at.count(T, T))
                    load_ordered(x[bass.ds(at.plus(1).index(), 1)].rearrange("o s d -> (o s) d"))
                elif kind == "load_v":
                    sp.wait_ge(values_done, at.count(USES * T, USES * T))
                    sp.dma_start(v_ctx[:], ctx[bass.ds(at.plus(1).index(), 1), :, D:2 * D].rearrange(
                        "o (t p) d -> p (o t) d", p=P)).then_inc(v_in, 16)
                elif kind == "stack_proj":
                    need(sp, b_filled, at.count(USES * UNITS, USES * UNITS))
                    sp.dma_start(k_stack[96:97], row_consts[0:1].rearrange("r (g j s) -> r g j s", g=G, j=HG)
                                 ).then_inc(k_stacked, 16)
                    sp.wait_ge(side_free, side("v", T - 1, at) + 1)
                    fill_stack(k_stack, pqT, K_PARTS, k_stacked)
                    fill_stack(q_stack, pqT, Q_PARTS, q_stacked)
                elif kind == "shift_row":
                    _, x_, g = step
                    key = ("shift", x_, g)
                    sp.wait_ge(work_free[w.bank(key)], w.released(key, at))
                    row = SHIFT_ROW[x_]
                    sp.dma_start(q_stack[row:row + 1, g, :, :], shift_row[:, :]).then_inc(shift_in, 16)
                elif kind == "keys":
                    g = step[1]
                    sp.wait_ge(key_lo, at.count(G, g + 1))
                    nb, ng = (at, g + 1) if g + 1 < G else (at.plus(1), 0)
                    if nb.reg is not None or nb.off < B:
                        load_keys(nb, ng)
                elif kind == "stack_keys":
                    groups = step[1]
                    sp.wait_ge(b_filled, at.count(USES * UNITS, (groups[-1] + 1) * UNITS))
                    sp.wait_ge(key_lo, at.count(G, groups[-1] + 1))
                    done = last_stacked if groups[-1] == G - 1 else k_stacked
                    fill_stack(k_stack, pqT, K_PARTS, done, groups)
                    for g in groups:
                        sp.dma_start(k_stack[96:99, g, :, :], key_rows[bass.ds(at.index(), 1)].rearrange(
                            "o r s -> (o r) s").unsqueeze(1).broadcast_to([3, HG, S])).then_inc(done, 16)
                elif kind == "queries":
                    sp.wait_ge(side_free, side("norm2", T - 1, at) + 1)
                    fill_stack(q_stack, actT, Q_PARTS, q_stacked)
                    sp.dma_start(q_stack[96:99], row_consts[0:3].rearrange("r (g j s) -> r g j s", g=G, j=HG)
                                 ).then_inc(q_stacked, 16)
                elif kind == "down_add":
                    _, hf, t = step
                    key = ("down", hf, t)
                    sp.wait_ge(work_free[w.bank(key)], w.released(key, at))
                    sp.dma_start(out.rearrange("b s d -> (b s) d")[bass.ds(at.plus(-1).count(S, P * t), P), :],
                                 res2[:, t, :]).then_inc(stored, 16)
                elif kind == "weights":
                    c = step[1]
                    need(sp, w_int, c - 1)
                    src, k = divmod(c, KD)
                    if src < 2:
                        sp.dma_start(w_raw[:, c % 2], (wgT, wuT)[src][P * k:P * (k + 1), :]).then_inc(wraw_in[c % 2], 16)
                    else:
                        sp.dma_start(w_raw[:, c % 2].rearrange("p (m n) -> p m n", n=D),
                                     wdT[3 * P * k:3 * P * (k + 1), :].rearrange("(m p) n -> p m n", p=P)
                                     ).then_inc(wraw_in[c % 2], 16)
            walk(sp, do)
            sp.wait_ge(stored, 16 * T * B)
            sp.wait_ge(rows_out, 16)

        @block.tensor
        def _(pe):
            pe.wait_ge(consts_made, 6)
            pe.wait_ge(row99_in, 16)

            def do(step, at, w):
                kind = step[0]

                def claim(key):
                    need(pe, work_free[w.bank(key)], w.free(key, at))
                    return work[:, w.bank(key), :]

                def claim_side(kind_, t):
                    need(pe, side_free, side(kind_, t, at) - 1)
                    if at.reg is not None or at.off >= 0:
                        pe.wait_ge(max_done, at.count(USES * UNITS, G * UNITS * (1 if kind_ == "norm2" else 2)))
                    return score_a[:, t % 2, :]

                def written(keys, claimed):
                    last = {w.bank(k): k for k in keys}
                    for bank, k in last.items():
                        if bank != w.bank(claimed):
                            pe.wait_ge(work_free[bank], w.released(k, at))

                if kind == "norm":
                    _, ln, t = step
                    bank = claim_side(f"norm{ln}", t)
                    la = ln_at(ln, at)
                    pe.wait_ge(normed[ln], la.count(T, t + 1))
                    for k in range(KD):
                        last = nc.tensor.transpose(bank[:, P * k:P * (k + 1)], xn[:, t % 2 + 2 * (ln == 3), P * k:P * (k + 1)], ident[:])
                    last.then_inc(norm_t[ln], 1)
                elif kind == "proj":
                    t = step[1]
                    bank = claim(step)
                    if t == 0:
                        need(pe, w_lo, 1)
                    pe.wait_ge(side_free, side("norm1", t, at) + 1)
                    n = 0
                    for k in range(KD):
                        for a, c in ((0, 0), (0, 1), (1, 0)):
                            last = nc.tensor.matmul(bank, actT[:, a, k, P * t:P * (t + 1)], wv[:, c, k, :],
                                                    start=n == 0, stop=n == 3 * KD - 1)
                            n += 1
                    last.then_inc(proj_done, 1)
                elif kind == "proj_t":
                    t = step[1]
                    bank = claim_side("v", t)
                    pe.wait_ge(v_made, at.plus(1).count(T, t + 1))
                    for g in range(G):
                        last = nc.tensor.transpose(bank[:, P * g:P * (g + 1)], v_self[:, t, P * g:P * (g + 1)], ident[:])
                    last.then_inc(projt_done, 1)
                elif kind == "maxima":
                    _, x_, a = step
                    g, j, t = a // UNITS, a % UNITS // T, a % T
                    n = G * UNITS * x_ + a
                    if a == 0:
                        pe.wait_ge(*q_ready(x_, at))
                        pe.wait_ge(*k_ready(x_, at))
                        need(pe, side_free, side_before(x_, at))
                    if a == 3 * UNITS and x_ == CA:
                        pe.wait_ge(last_stacked, at.count(BLOCKS + 16, BLOCKS + 16))
                    need(pe, max_done, at.count(USES * UNITS, n - 1))
                    nc.tensor.matmul(score_a[:, n % 2, :], q_stack[0:K_MAX[x_], g, j, P * t:P * (t + 1)],
                                     k_stack[0:K_MAX[x_], g, j, :], start=True, stop=True).then_inc(a_filled, 1)
                elif kind == "shift":
                    _, x_, g = step
                    u = G * x_ + g
                    bank = claim(step)
                    pe.wait_ge(max_done, at.count(USES * UNITS, (u + 1) * UNITS))
                    for t in range(T):
                        last = nc.tensor.transpose(bank[0:HG, P * t:P * (t + 1)], negmax[:, g % 2, t, :], ident[:])
                    last.then_inc(shift_t, 1)
                elif kind == "probs":
                    _, x_, n = step
                    g, kt, j = n // UNITS, n % UNITS // HG, n % HG
                    n += G * UNITS * x_
                    rows = SHIFT_ROW[x_] + 1
                    if n % UNITS == 0:
                        pe.wait_ge(shift_in, at.count(16 * USES, 16 * (n // UNITS + 1)))
                    need(pe, exp_done, at.count(USES * UNITS, n - 2 if n > 1 else n - 1))
                    nc.tensor.matmul(score_b[:, n % 3, :], k_stack[0:rows, g, j, P * kt:P * (kt + 1)],
                                     q_stack[0:rows, g, j, :], start=True, stop=True).then_inc(b_filled, 1)
                elif kind == "values":
                    _, x_, g, kt = step
                    u = G * x_ + g
                    v = v_self if x_ == SA else v_ctx
                    if kt == 0:
                        need(pe, attn_out, at.count(USES, u))
                        if x_ == CA and g == 0:
                            pe.wait_ge(v_in, at.count(16, 16))
                    pe.wait_ge(exp_done, at.count(USES * UNITS, u * UNITS + (kt + 1) * HG))
                    for j in range(HG):
                        h = g * HG + j
                        if x_ == CA:
                            last = nc.tensor.matmul(attn[DH * j:DH * (j + 1), :], v[:, kt, DH * h:DH * (h + 1)],
                                                    probs[:, kt, j, :], start=kt == 0, stop=kt == T - 1)
                        else:
                            for i in range(T):
                                last = nc.tensor.matmul(attn[DH * i:DH * (i + 1), P * j:P * (j + 1)],
                                                        v[:, kt, DH * h:DH * (h + 1)],
                                                        probs[:, kt, j, P * i:P * (i + 1)],
                                                        start=kt == 0 and j == 0, stop=kt == T - 1 and j == HG - 1,
                                                        skip_group_check=True)
                    last.then_inc(values_done, 1)
                elif kind == "denom":
                    _, x_, g, parts = step
                    u = G * x_ + g
                    key = ("denom", x_, g)
                    bank = work[:, w.bank(key), :]
                    for half in parts:
                        if half == 0:
                            claim(key)
                        pe.wait_ge(sums, at.count(4 * USES, 4 * u + 2 + 2 * half))
                        slot = 1 + 2 * half
                        for j in range(HG):
                            if x_ == CA:
                                last = nc.tensor.matmul(bank[DH * j:DH * (j + 1), :], ones[:], probs[:, slot, j, :],
                                                        start=half == 0, stop=half == 1)
                            else:
                                for i in range(T):
                                    last = nc.tensor.matmul(bank[DH * i:DH * (i + 1), P * j:P * (j + 1)], ones[:],
                                                            probs[:, slot, j, P * i:P * (i + 1)],
                                                            start=half == 0 and j == 0, stop=half == 1 and j == HG - 1,
                                                            skip_group_check=True)
                        last.then_inc(denom_done, 1)
                elif kind == "back_d":
                    g = step[1]
                    bank = claim(step)
                    written([("denom", CA, g)], step)
                    for t in range(T):
                        last = nc.tensor.transpose(bank[:, P * t:P * (t + 1)], den[:, P * t:P * (t + 1)], ident[:])
                    last.then_inc(back_d, 1)
                elif kind == "back_o":
                    g = step[1]
                    bank = claim(step)
                    pe.wait_ge(attn_out, at.count(USES, G + g + 1))
                    for t in range(T):
                        last = nc.tensor.transpose(bank[:, P * t:P * (t + 1)], attn_raw[:, g % 2, P * t:P * (t + 1)], ident[:])
                    last.then_inc(back_o, 1)
                elif kind == "out_proj":
                    t = step[1]
                    bank = claim(step)
                    pe.wait_ge(div_used, at.count(USES, t + 1))
                    if t == 0:
                        need(pe, w_lo, 2)
                    n = 0
                    for k in range(KD):
                        for a, c in ((0, 0), (0, 1), (1, 0)):
                            last = nc.tensor.matmul(bank, actT[:, a, k, P * t:P * (t + 1)], wo[:, c, k, :],
                                                    start=n == 0, stop=n == 3 * KD - 1)
                            n += 1
                    last.then_inc(outproj_done, 1)
                elif kind == "gate_up":
                    _, hf, m = step
                    bank = claim(step)
                    if m == 0:
                        pe.wait_ge(side_free, side("norm3", 2 * hf + 1, gu_at(hf, at)) + 1)
                        need(pe, w_int, 2 * KD)
                    for half, wt in enumerate((wg, wu)):
                        for k in range(KD):
                            for a in (0, 1):
                                last = nc.tensor.matmul(bank[:, HALF * half:HALF * (half + 1)], wt[:, k, P * m:P * (m + 1)],
                                                        x3T[:, a, k, :], start=k == 0 and a == 0, stop=k == KD - 1 and a == 1)
                    last.then_inc(gu_filled, 1)
                elif kind == "down":
                    _, hf, t, parts = step
                    key = ("down", hf, t)
                    bank = work[:, w.bank(key), :]
                    ma = at.plus(-1)
                    if parts[0] == 0:
                        claim(key)
                        if hf == 0 and t == 0:
                            need(pe, w_int, 3 * KD)
                    tt = t - 2 * hf
                    for m in parts:
                        if t % 2 == 0 and m in (0, MH - 2):
                            pe.wait_ge(hid_lo, ma.count(2 * MH, MH * hf + (m or MH - 2) + 2 * (m > 0)))
                        for a in (0, 1):
                            last = nc.tensor.matmul(bank, hid[:, a, m, P * tt:P * (tt + 1)], wd[:, m, :],
                                                    start=m == 0 and a == 0, stop=m == MH - 1 and a == 1)
                    if parts[-1] == MH - 1:
                        last.then_inc(down_done, 1)
            walk(pe, do)

        @block.scalar
        def _(act):
            for n, (raw, parts) in enumerate(((wv_raw, wv), (wo_raw, wo))):
                act.wait_ge(wraw_in[n], 16)
                nc.scalar.activation(parts[:, 0], raw, ACT.Copy, scale=SW).then_inc(w_hi, 1)

            def hidden_hi(hf, m, at, w):
                key = ("gate_up", hf, m)
                act.wait_ge(work_free[w.bank(key)], w.released(key, at))
                nc.scalar.activation(hid[:, 0, m, :], hraw[:, m % 2, :], ACT.Copy).then_inc(hid_hi, 1)

            def do(step, at, w):
                kind = step[0]
                if kind == "norm":
                    _, ln, t = step
                    la = ln_at(ln, at)
                    act.wait_ge(norm_t[ln], la.count(T, t + 1))
                    src = score_a[:, t % 2, :].rearrange("p (k s) -> p k s", k=KD)
                    if ln == 3:
                        dst = x3T[:, 0, :, P * (t % 2):P * (t % 2 + 1)]
                    else:
                        dst = actT[:, 0, :, P * t:P * (t + 1)]
                    nc.scalar.activation(dst, src, ACT.Copy, scale=SX).then_inc(norm_hi[ln], 1)
                elif kind == "proj_t":
                    t = step[1]
                    act.wait_ge(projt_done, at.plus(1).count(T, t + 1))
                    nc.scalar.activation(pqT[:, 0, :, P * t:P * (t + 1)],
                                         score_a[:, t % 2, :].rearrange("p (k s) -> p k s", k=KD), ACT.Copy,
                                         scale=SP_).then_inc(projt_hi, 1)
                elif kind == "shift_row":
                    _, x_, g = step
                    u = G * x_ + g
                    key = ("shift", x_, g)
                    need(act, shift_in, at.count(16 * USES, 16 * u))
                    act.wait_ge(shift_t, at.count(USES, u + 1))
                    nc.scalar.activation(shift_row[:], work[0:HG, w.bank(key), :], ACT.Copy,
                                         scale=1.0 / (SHIFT_SA, SHIFT_CA)[x_]).then_inc(work_free[w.bank(key)], 1)
                elif kind == "probs":
                    _, x_, n = step
                    kt, j = n % UNITS // HG, n % HG
                    n += G * UNITS * x_
                    u = n // UNITS
                    if kt % 2 == 0 and j % 2 == 0:
                        need(act, sums, at.count(4 * USES, 4 * (u - 1) + kt + j // 2 + 1))
                    elif kt % 2 and j == 0:
                        need(act, denom_done, at.count(2 * USES, 2 * (u - 1) + 1 + kt // 2))
                    act.wait_ge(b_filled, at.count(USES * UNITS, n + 1))
                    nc.scalar.activation(probs[:, kt, j, :], score_b[:, n % 3, :], ACT.Exp,
                                         scale=(1.0 / (SP_ * SP_ * DH ** 0.5), 1.0 / CA_SCORE)[x_]).then_inc(exp_done, 1)
                elif kind == "evacuate":
                    _, x_, g = step
                    u = G * x_ + g
                    if (u - 2) % USES < G:
                        need(act, div_done, at.count(G, g - 1 if x_ == SA else G - 1 + g))
                    else:
                        need(act, back_o, at.count(G, g - 1 if x_ == CA else g - G + G - 1))
                    act.wait_ge(values_done, at.count(USES * T, T * (u + 1)))
                    nc.scalar.activation(attn_raw[:, g % 2, :], attn[:], ACT.Copy,
                                         scale=(SP_, 1.0)[x_]).then_inc(attn_out, 1)
                elif kind == "den_copy":
                    g = step[1]
                    key = ("denom", CA, g)
                    act.wait_ge(denom_done, at.count(2 * USES, 2 * (G + g + 1)))
                    need(act, back_d, at.count(G, g))
                    nc.scalar.activation(den[:], work[:, w.bank(key), :], ACT.Copy).then_inc(work_free[w.bank(key)], 1)
                elif kind == "fold":
                    g = step[1]
                    act.wait_ge(div_done, at.count(G, g + 1))
                    nc.scalar.activation(folded(0, g), attn_div[:].rearrange("p (j k b) -> p j k b", j=HG, k=KD),
                                         ACT.Copy).then_inc(div_hi, 1)
                elif kind == "keys":
                    g = step[1]
                    act.wait_ge(key_in, at.count(16 * G, 16 * (g + 1)))
                    if g == 0:
                        act.wait_ge(*q_ready(SA, at))
                        act.wait_ge(*k_ready(SA, at))
                    nc.scalar.activation(pqT[:, 0, g, :], keyT[:], ACT.Copy, scale=SP_).then_inc(key_hi, 1)
                elif kind == "silu":
                    _, hf, m = step
                    ma = gu_at(hf, at)
                    act.wait_ge(gu_filled, ma.count(2 * MH, MH * hf + m + 1))
                    nc.scalar.activation(th[:, m % 2, :], work[:, w.bank(("gate_up", hf, m)), 0:HALF], ACT.Tanh,
                                         scale=0.5 * DEQ / SX).then_inc(tanh_done, 1)
                    if m:
                        hidden_hi(hf, m - 1, at, w)
                elif kind == "hidden_end":
                    hidden_hi(step[1], MH - 1, at, w)
                elif kind == "to_half":
                    c = step[1]
                    act.wait_ge(wraw_in[c % 2], 16 + 16 * (c // 2 + 1))
                    src, k = divmod(c, KD)
                    dst = (wg[:, k, :], wu[:, k, :], wd[:, 3 * k:3 * (k + 1), :].rearrange("p m n -> p (m n)"))[src]
                    nc.scalar.activation(dst, w_raw[:, c % 2], ACT.Copy).then_inc(w_int, 1)
            walk(act, do)

        @block.vector
        def _(dve):
            for n, (raw, parts) in enumerate(((wv_raw, wv), (wo_raw, wo))):
                dve.wait_ge(w_hi, n + 1)
                nc.vector.scalar_tensor_tensor(parts[:, 1].rearrange("p k e -> p (k e)"), raw.rearrange("p k e -> p (k e)"),
                                               SW, parts[:, 0].rearrange("p k e -> p (k e)"),
                                               ALU.mult, ALU.subtract).then_inc(w_lo, 1)
                if n == 0:
                    dve.wait_ge(consts_in, 16 * 6)
                    nc.vector.tensor_copy(len8f, len8i).then_inc(table_step, 1)
                    dve.wait_ge(table_step, 1)
                    nc.vector.tensor_scalar(gate8, len8f, 0.0, None, ALU.is_gt).then_inc(table_step, 1)
                    dve.wait_ge(table_step, 2)
                    nc.vector.tensor_scalar(inv8, pos8, len8f, gate8, ALU.is_ge, ALU.mult).then_inc(table_step, 1)
                    dve.wait_ge(table_step, 3)
                    nc.vector.tensor_scalar(rows8[:, 2], inv8, -65504.0, None, ALU.mult).then_inc(table_step, 1)
                    nc.vector.tensor_scalar(bias8, bias8, gate8, SP_, ALU.mult, ALU.mult).then_inc(table_step, 1)
                    dve.wait_ge(table_step, 5)
                    nc.vector.tensor_copy(rows8[:, 0], bias8).then_inc(table_step, 1)
                    dve.wait_ge(table_step, 6)
                    nc.vector.tensor_tensor(rows8[:, 1], bias8, rows8[:, 0], ALU.subtract).then_inc(table_step, 1)
                    nc.vector.tensor_copy(gate[:], lens_i[:]).then_inc(table_step, 1)
                    dve.wait_ge(table_step, 8)
                    nc.vector.tensor_scalar(gate[:], gate[:], 0.0, DH ** -0.5, ALU.is_gt, ALU.mult).then_inc(table_step, 1)

            def do(step, at, w):
                kind = step[0]
                if kind == "stats":
                    _, ln, t = step
                    la = ln_at(ln, at)
                    if ln == 1:
                        dve.wait_ge(xin_in, la.count(16 * KD, 16 * KD))
                        src = xin
                    elif ln == 2:
                        key = ("out_proj", t)
                        dve.wait_ge(work_free[w.bank(key)], w.released(key, at))
                        src = res1
                    else:
                        dve.wait_ge(div_used, la.count(USES, USES))
                        src = res2
                    nc.vector.bn_stats(bst[:, ln - 1, t, :], src[:, t, :]).then_inc(stat[ln], 1)
                elif kind == "rstd":
                    _, ln, tiles = step
                    la = ln_at(ln, at)
                    dve.wait_ge(stat[ln], la.count(T, tiles[-1] + 1))
                    nc.vector.memset(carrier[:], 0.0)
                    for t in tiles:
                        nc.vector.bn_aggr(mv[:, ln - 1, t, :], bst[:, ln - 1, t, :]).then_inc(meanvar[ln], 1)
                elif kind == "scale":
                    _, ln, t = step
                    la = ln_at(ln, at)
                    dve.wait_ge(rstd[ln], la.count(*rstd_ops(ln, (3,) if ln == 1 else (t,))))
                    if t >= 2:
                        dve.wait_ge(norm_t[ln], la.count(T, t - 1))
                    nc.vector.tensor_scalar(xn[:, t % 2 + 2 * (ln == 3), :], (xin, res1, res2)[ln - 1][:, t, :],
                                            mv[:, ln - 1, t, 0:1], rs[:, ln - 1, t:t + 1],
                                            ALU.subtract, ALU.mult).then_inc(normed[ln], 1)
                elif kind == "norm_lo":
                    _, ln, t = step
                    la = ln_at(ln, at)
                    dve.wait_ge(norm_hi[ln], la.count(T, t + 1))
                    src = score_a[:, t % 2, :].rearrange("p (k s) -> p k s", k=KD)
                    buf, col = (x3T, t % 2) if ln == 3 else (actT, t)
                    nc.vector.scalar_tensor_tensor(buf[:, 1, :, P * col:P * (col + 1)], src, SX,
                                                   buf[:, 0, :, P * col:P * (col + 1)],
                                                   ALU.mult, ALU.subtract).then_inc(side_free, 1)
                elif kind == "proj_add":
                    t = step[1]
                    bank = w.bank(("proj", t))
                    dve.wait_ge(proj_done, at.plus(1).count(T, t + 1))
                    nc.vector.scalar_tensor_tensor(v_self[:, t, :], work[:, bank, :], 1.0 / (SX * SW), bvb[:],
                                                   ALU.mult, ALU.add).then_inc(work_free[bank], 1)
                    dve.wait_ge(work_free[bank], w.released(("proj", t), at))
                    nc.vector.memset(carrier[:], 0.0).then_inc(v_made, 1)
                elif kind == "proj_lo":
                    t = step[1]
                    dve.wait_ge(projt_hi, at.plus(1).count(T, t + 1))
                    nc.vector.scalar_tensor_tensor(pqT[:, 1, :, P * t:P * (t + 1)],
                                                   score_a[:, t % 2, :].rearrange("p (k s) -> p k s", k=KD), SP_,
                                                   pqT[:, 0, :, P * t:P * (t + 1)],
                                                   ALU.mult, ALU.subtract).then_inc(side_free, 1)
                elif kind == "maxima":
                    _, x_, a = step
                    g, j, t = a // UNITS, a % UNITS // T, a % T
                    n = G * UNITS * x_ + a
                    if a % UNITS == 0:
                        need(dve, shift_t, at.count(USES, n // UNITS - 1))
                    dve.wait_ge(a_filled, at.count(USES * UNITS, n + 1))
                    nc.vector.tensor_reduce(negmax[:, g % 2, t, j:j + 1], score_a[:, n % 2, :], AX_X, ALU.max,
                                            negate=True).then_inc(max_done, 1)
                elif kind == "divide":
                    _, g, quarters = step
                    bank = w.bank(("denom", SA, g))
                    if quarters[0] == 0:
                        need(dve, div_done, at.count(G, g))
                        dve.wait_ge(denom_done, at.count(2 * USES, 2 * (g + 1)))
                    for q in quarters:
                        last = nc.vector.reciprocal(den[:, P * q:P * (q + 1)], work[:, bank, P * q:P * (q + 1)])
                    if q == T - 1:
                        last.then_inc(work_free[bank], 1)
                elif kind == "back_r":
                    g = step[1]
                    bank = w.bank(("back_d", g))
                    dve.wait_ge(back_d, at.count(G, g + 1))
                    nc.vector.reciprocal(rcol[:], work[:, bank, :].rearrange("p (n i) -> p n i", i=DH)[:, :, 0]
                                         ).then_inc(work_free[bank], 1)
                elif kind == "back_add":
                    g = step[1]
                    kd, ko = ("back_d", g), ("back_o", g)
                    dve.wait_ge(back_o, at.count(G, g + 1))
                    dve.wait_ge(work_free[w.bank(kd)], w.released(kd, at))
                    need(dve, div_used, at.count(USES, G + g))
                    nc.vector.tensor_tensor(attn_div[:].rearrange("p (n i) -> p n i", i=DH),
                                            work[:, w.bank(ko), :].rearrange("p (n i) -> p n i", i=DH),
                                            rcol[:].unsqueeze(2).broadcast_to([P, T * HG, DH]),
                                            ALU.mult).then_inc(work_free[w.bank(ko)], 1)
                elif kind == "out_add":
                    t = step[1]
                    bank = w.bank(("out_proj", t))
                    dve.wait_ge(outproj_done, at.count(T, t + 1))
                    if t == 0:
                        dve.wait_ge(bo_added, at.count(1, 1))
                    nc.vector.scalar_tensor_tensor(res1[:, t, :], work[:, bank, :], 1.0 / (SP_ * SW), res1[:, t, :],
                                                   ALU.mult, ALU.add).then_inc(work_free[bank], 1)
                elif kind == "keys":
                    g = step[1]
                    dve.wait_ge(key_hi, at.count(G, g + 1))
                    nc.vector.scalar_tensor_tensor(pqT[:, 1, g, :], keyT[:], SP_, pqT[:, 0, g, :],
                                                   ALU.mult, ALU.subtract).then_inc(key_lo, 1)
                elif kind == "silu":
                    _, hf, m = step
                    ma = gu_at(hf, at)
                    n = MH * hf + m
                    bank = work[:, w.bank(("gate_up", hf, m)), :]
                    dve.wait_ge(tanh_done, ma.count(2 * MH, n + 1))
                    nc.vector.scalar_tensor_tensor(th[:, m % 2, :], th[:, m % 2, :], 1.0, bank[:, 0:HALF],
                                                   ALU.add, ALU.mult).then_inc(silu_done, 1)
                    dve.wait_ge(silu_done, ma.count(2 * MH, n + 1))
                    need(dve, hid_lo, ma.count(2 * MH, n - 1))
                    nc.vector.scalar_tensor_tensor(hraw[:, m % 2, :], th[:, m % 2, :], 0.5 * SHID * (DEQ / SX) ** 2,
                                                   bank[:, HALF:2 * HALF], ALU.mult, ALU.mult
                                                   ).then_inc(work_free[w.bank(("gate_up", hf, m))], 1)
                elif kind == "down_add":
                    _, hf, t = step
                    bank = w.bank(("down", hf, t))
                    dve.wait_ge(down_done, at.plus(-1).count(T, t + 1))
                    nc.vector.scalar_tensor_tensor(res2[:, t, :], work[:, bank, :], DEQ / SHID, res2[:, t, :],
                                                   ALU.mult, ALU.add).then_inc(work_free[bank], 1)
            walk(dve, do)

        @block.gpsimd
        def _(pool):
            nc.gpsimd.memset(ident[:], 0.0).then_inc(consts_made, 1)
            pool.wait_ge(consts_made, 1)
            nc.gpsimd.affine_select(out=ident[:], in_=ident[:], compare_op=ALU.not_equal, fill=1.0, base=0,
                                    pattern=[[-1, P]], channel_multiplier=1).then_inc(consts_made, 1)
            nc.gpsimd.memset(ones[:], 1.0).then_inc(consts_made, 1)
            nc.gpsimd.memset(powers[:, 0, :], EPS).then_inc(consts_made, 1)
            nc.gpsimd.memset(powers[:, 1, :], -0.5).then_inc(consts_made, 1)
            nc.gpsimd.memset(rcol[:], 1.0).then_inc(consts_made, 1)
            pool.wait_ge(consts_made, 6)

            def hidden_lo(hf, m, at):
                pool.wait_ge(hid_hi, gu_at(hf, at).count(2 * MH, MH * hf + m + 1))
                nc.gpsimd.tensor_tensor(hid[:, 1, m, :], hraw[:, m % 2, :], hid[:, 0, m, :],
                                        ALU.subtract).then_inc(hid_lo, 1)

            def do(step, at, w):
                kind = step[0]
                if kind == "rstd":
                    _, ln, tiles = step
                    a, b = tiles[0], tiles[-1] + 1
                    la = ln_at(ln, at)
                    per, n = rstd_ops(ln, tiles)
                    n -= 3 if ln == 2 else 2
                    r = rs[:, ln - 1, a:b]
                    pool.wait_ge(meanvar[ln], la.count(T, b))
                    nc.gpsimd.tensor_tensor(r, mv[:, ln - 1, a:b, 1], powers[:, 0, a:b], ALU.add).then_inc(rstd[ln], 1)
                    pool.wait_ge(rstd[ln], la.count(per, n + 1))
                    nc.gpsimd.tensor_tensor(r, r, powers[:, 1, a:b], ALU.pow).then_inc(rstd[ln], 1)
                    if ln == 2:
                        pool.wait_ge(rstd[ln], la.count(per, n + 2))
                        if at.reg is None and at.off == 0:
                            pool.wait_ge(table_step, 9)
                        nc.gpsimd.tensor_tensor(carrier_pool[:], powers[:, 0, 0:1], powers[:, 1, 0:1], ALU.add)
                        nc.gpsimd.tensor_tensor(r, r, gate[:, bass.ds(at.index(), 1)],
                                                ALU.mult).then_inc(rstd[ln], 1)
                elif kind == "add_bo":
                    la = at.plus(1)
                    pool.wait_ge(x_in, la.count(16, 16))
                    if at.reg is None and at.off == -1:
                        pool.wait_ge(consts_in, 16 * 6)
                    nc.gpsimd.tensor_tensor(res1[:], res1[:], bob[:].unsqueeze(1).broadcast_to([P, T, D]),
                                            ALU.add).then_inc(bo_added, 1)
                elif kind == "values" and step[3] % 2:
                    _, x_, g, kt = step
                    u = G * x_ + g
                    pool.wait_ge(values_done, at.count(USES * T, T * u + kt + 1))
                    for j in (0, 2):
                        nc.gpsimd.tensor_tensor(probs[:, kt, j:j + 2], probs[:, kt - 1, j:j + 2],
                                                probs[:, kt, j:j + 2], ALU.add).then_inc(sums, 1)
                elif kind == "divide" and step[2][-1] == T - 1:
                    g = step[1]
                    key = ("denom", SA, g)
                    pool.wait_ge(work_free[w.bank(key)], w.released(key, at))
                    pool.wait_ge(attn_out, at.count(USES, g + 1))
                    need(pool, div_used, at.count(USES, g))
                    nc.gpsimd.tensor_tensor(attn_div[:], attn_raw[:, g % 2, :], den[:], ALU.mult).then_inc(div_done, 1)
                elif kind == "fold":
                    g = step[1]
                    pool.wait_ge(div_hi, at.count(G, g + 1))
                    nc.gpsimd.tensor_tensor(folded(1, g), attn_div[:].rearrange("p (j k b) -> p j k b", j=HG, k=KD),
                                            folded(0, g),
                                            ALU.subtract).then_inc(div_used, 1)
                elif kind == "back_add":
                    g = step[1]
                    key = ("back_o", g)
                    if g == 0:
                        need(pool, stored, at.count(16 * T, 0))
                    pool.wait_ge(work_free[w.bank(key)], w.released(key, at))
                    nc.gpsimd.tensor_tensor(res2[:, :, P * g:P * (g + 1)], res1[:, :, P * g:P * (g + 1)],
                                            attn_div[:].rearrange("p (t e) -> p t e", t=T),
                                            ALU.add).then_inc(div_used, 1)
                elif kind == "silu" and step[2]:
                    hidden_lo(step[1], step[2] - 1, at)
                elif kind == "hidden_end":
                    hidden_lo(step[1], MH - 1, at)
            walk(pool, do)


def kernel(x, ctx_2048, itok_Bx1_68_817, L0_attn_Wv, L0_attn_bv, L0_attn_Wo, L0_attn_bo, L0_xattn_b,
           L0_ffn_w_gate, L0_ffn_w_up, L0_ffn_w_down):
    import concourse.bacc as bacc
    from concourse.bass_utils import run_bass_kernel_spmd

    ctx = np.ascontiguousarray(ctx_2048)
    arrays = {
        "x": np.ascontiguousarray(x),
        "ctx": ctx,
        "ctx_kT": np.ascontiguousarray(ctx[:, :, :D].transpose(0, 2, 1)),
        "lens": np.ascontiguousarray(itok_Bx1_68_817),
        "wvT": np.ascontiguousarray(np.asarray(L0_attn_Wv).T),
        "bv": np.ascontiguousarray(L0_attn_bv),
        "woT": np.ascontiguousarray(np.asarray(L0_attn_Wo).T),
        "bo": np.ascontiguousarray(L0_attn_bo),
        "key_bias": np.ascontiguousarray(L0_xattn_b),
        "wgT": np.ascontiguousarray(np.asarray(L0_ffn_w_gate).T),
        "wuT": np.ascontiguousarray(np.asarray(L0_ffn_w_up).T),
        "wdT": np.ascontiguousarray(np.asarray(L0_ffn_w_down).T),
        "positions": np.arange(S, dtype=np.float32)[None, :],
        "row_consts": np.repeat(np.array([[1024.0], [1024.0], [32768.0], [16384.0]], np.float16), H * S, axis=1),
    }
    nc = bacc.Bacc("TRN2", target_bir_lowering=False, num_devices=1,
                   dynamic_dma_scratch_size=1024)
    args = [nc.dram_tensor(f"in_{n}", a.shape, mybir.dt.from_np(a.dtype), kind="ExternalInput").ap()
            for n, a in arrays.items()]
    out = nc.dram_tensor("out", (B, S, D), F32, kind="ExternalOutput").ap()
    build(nc, *args, out)
    r = run_bass_kernel_spmd(nc, [{f"in_{n}": a for n, a in arrays.items()}], core_ids=[0])
    return r.results[0]["out"]
```

```python
from contextlib import ExitStack

import numpy as np

import concourse.bass as bass
from concourse import mybir

F32 = mybir.dt.float32
F16 = mybir.dt.float16
I32 = mybir.dt.int32
ALU = mybir.AluOpType
ACT = mybir.ActivationFunctionType
AX_X = mybir.AxisListType.X

P = 128
B, S, D, H = 8, 512, 512, 16
DH = D // H
T = S // P
KD = D // P
G = 4
HG = H // G
HID = 1536
MH = HID // P
HALF = S // 2
EPS = 1e-5

SX = 1024.0
SW = 64.0
SP_ = 16.0
SHID = 0.125
DEQ = 1.0 / 127.0
CA_SCORE = SX * SP_
SHIFT_SA, SHIFT_CA = 1024.0, 16384.0
SA, CA = 0, 1
K_MAX = {SA: 3 * DH, CA: 3 * DH + 3}
SHIFT_ROW = {SA: 3 * DH, CA: 3 * DH + 3}
USES = 2 * G
UNITS = T * HG

LEAD = 23
LAG = 2
DENOM1, DENOM2 = 3, 10
KEYS_AT = (8, 37, 45, 60)
BESIDE_MID = 12
LATER = 4
WEIGHTS_AT = -5
FIRST_CHUNKS = 8


class At:

    def __init__(self, reg, off=0):
        self.reg, self.off = reg, off

    def plus(self, n):
        return At(self.reg, self.off + n)

    def count(self, per_batch, within):
        fixed = self.off * per_batch + within
        return fixed if self.reg is None else self.reg * per_batch + fixed

    def index(self):
        return self.off if self.reg is None else self.reg + self.off


class Work:

    def __init__(self, steps, before, first):
        self.number, self.before, self.first = {}, before, first
        for step in steps:
            for key in work_units(step):
                self.number[key] = len(self.number)
        self.units = len(self.number)

    def bank(self, key):
        return self.number[key] % 2

    def released(self, key, at):
        n = self.before + self.number[key]
        base = n // 2 + 1
        return at.plus(-self.first).count(self.units // 2, base)

    def free(self, key, at):
        n = self.before + self.number[key]
        return at.plus(-self.first).count(self.units // 2, n // 2)


def work_units(step):
    kind = step[0]
    if kind in ("denom", "down"):
        return [step[:3]] if step[3][0] == 0 else []
    if kind in ("proj", "out_proj", "shift", "back_d", "back_o", "gate_up"):
        return [step]
    return []


def norm_piece(ln, t):
    return [("norm", ln, t), ("norm_lo", ln, t)]


def stats_pieces(ln, tiles):
    return [[("stats", ln, t)] for t in tiles] + [[("rstd", ln, tiles)]]


def project_pieces():
    return [[("proj", t), ("proj_add", t)] for t in range(T)] + [[("proj_t", t), ("proj_lo", t)] for t in range(T)]


def out_piece(t):
    return [("out_proj", t), ("out_add", t)]


def gate_up_pieces(hf, a=0, b=MH):
    out = [[("gate_up", hf, m), ("silu", hf, m)] + ([("hidden", hf, m - 1)] if m > a else []) for m in range(a, b)]
    out[-1].append(("hidden", hf, b - 1))
    return out


def down_piece(hf, t):
    return [("down", hf, t, tuple(range(MH))), ("down_add", hf, t)]


def down_spread(hf, t):
    return [("down", hf, t, (m, m + 1)) for m in range(0, MH, 2)] + [("down_add", hf, t)]


def pipeline(pieces):
    out, late = [], []
    for p in pieces:
        if not p:
            out += late
            late = []
        elif len(p) == 1:
            out += p
        else:
            out += p[:1] + late
            late = p[1:]
    return out + late


def attention_steps(x, head, late, end):
    out, divides = [], {}
    for n in range(-LEAD, G * UNITS + LAG + 1):
        a = n + LEAD
        maxima = [("maxima", x, a)] if a < G * UNITS else []
        early = n % HG != (LAG - 1) % HG
        if early:
            out += maxima
        g, r = divmod(a - UNITS, UNITS)
        if r == 1 and 0 <= g < G:
            out.append(("shift", x, g))
        if r == 2 and 0 <= g < G:
            out.append(("shift_row", x, g))
        if 0 <= n < G * UNITS:
            out.append(("probs", x, n))
        if not early:
            out += maxima
        if n < 0:
            out += head[len(head) * a // LEAD:len(head) * (a + 1) // LEAD]
        g, r = divmod(n - LAG, UNITS)
        if r % HG == HG - 1 and 0 <= g < G:
            out.append(("values", x, g, r // HG))
        if r == 0 and 1 <= g <= G:
            out.append(("evacuate", x, g - 1))
        g, r = n // UNITS - 1, n % UNITS
        if 0 <= g < G - 1:
            if r == DENOM1:
                out.append(("denom", x, g, (0,)))
            elif r == DENOM2:
                out.append(("denom", x, g, (1,)))
                if x == SA:
                    divides = {n + 1 + q * (2 if g == 0 else 1): ("divide", g, (q,)) for q in range(T)}
            elif x == CA and r == DENOM2 + 1:
                out.append(("den_copy", g))
            elif x == CA and r > DENOM2 + 2:
                out += ([("back_d", g)], [("back_r", g), ("back_o", g)], [("back_add", g)])[r - DENOM2 - 3]
        if n in divides:
            out.append(divides.pop(n))
        if x == SA and r == 6 and 1 <= g <= G - 2:
            out.append(("fold", g - 1))
        if x == SA and n in KEYS_AT:
            out.append(("keys", KEYS_AT.index(n)))
        if x == SA and n == 3 * UNITS + 1:
            out.append(("stack_keys", (0, 1, 2)))
        out += late.get(n, [])
    return out + end


def add_weights(late, a, b):
    for i, c in enumerate(range(a, b)):
        n = WEIGHTS_AT + 8 * i
        late[n] = late.get(n, []) + [("weights", c)]
        late[n + 8] = late.get(n + 8, []) + [("to_half", c)]


def batch_steps(first, last):
    b = [[]] * MH if first else gate_up_pieces(1)
    late = {49: [("out_proj", 0)], 50: [("out_add", 0)], 52: [("stats", 2, 0)], 53: [("rstd", 2, [0])],
            56: [("scale", 2, 0)], 57: [("norm", 2, 0)], 58: [("norm_lo", 2, 0)], 64: [("out_proj", 1)],
            65: [("out_add", 1)]}
    if not first:
        late[0] = [("add_bo", 0)]
        late.update({41: [("scale", 3, 2)], 42: [("norm", 3, 2)], 43: [("scale", 3, 3)], 44: [("norm_lo", 3, 2)],
                     45: [("norm", 3, 3)], 46: [("norm_lo", 3, 3)]})
    if first:
        add_weights(late, 0, FIRST_CHUNKS)
    downs = [] if first else down_spread(1, 2) + down_spread(1, 3)
    end = pipeline(
        [[("fold", 2)]] + stats_pieces(2, [1])
        + b[:3] + [[("denom", SA, 3, (0, 1)), ("divide", 3, (0, 1, 2, 3))]]
        + [[("scale", 2, 1)], out_piece(2), norm_piece(2, 1)]
        + b[3:4] + [[("queries", 0)]] + stats_pieces(2, [2]) + [[("fold", 3)]] + b[4:5]
        + [out_piece(3), [("scale", 2, 2)]] + b[5:6] + [norm_piece(2, 2)] + stats_pieces(2, [3]) + b[6:7]
        + [[("scale", 2, 3)]] + b[7:8] + [norm_piece(2, 3)]
        + [[("queries", 1)], [("stack_keys", (3,))]] + b[8:BESIDE_MID])
    head = [] if last else [("load_ordered",)]
    before = [] if first else sum(gate_up_pieces(0, MH - LATER), []) + down_spread(0, 0) + down_spread(0, 1)
    out = head + before[:2] + attention_steps(SA, before[2:], late, end)
    late = {} if last else {
        40: [("stats", 1, 0)], 41: [("stats", 1, 1)], 44: [("stats", 1, 2)], 45: [("stats", 1, 3)],
        46: [("rstd", 1, [0, 1, 2, 3])], 48: [("scale", 1, 0)], 49: [("norm", 1, 0), ("scale", 1, 1)],
        50: [("norm_lo", 1, 0)], 51: [("norm", 1, 1)], 52: [("scale", 1, 2)], 53: [("norm_lo", 1, 1)],
        55: [("norm", 1, 2)], 56: [("scale", 1, 3)], 57: [("norm_lo", 1, 2)], 58: [("norm", 1, 3)],
        60: [("norm_lo", 1, 3)]}
    if first:
        add_weights(late, FIRST_CHUNKS, MH)
    pr = [] if last else project_pieces()
    gu = gate_up_pieces(0, 0, MH - LATER)
    load = [] if last else [[("stack_proj",)], [("load_x",)], [("load_v",)]]
    end = pipeline(
        pr[:2] + [[("denom", CA, 3, (0, 1)), ("den_copy", 3)]] + pr[4:6] + [[("back_d", 3), ("back_r", 3)]]
        + [[("back_o", 3), ("back_add", 3)]] + (pr[2:4] or [[]]) + stats_pieces(3, [0, 1]) + pr[6:7]
        + [[("scale", 3, 0)], [("scale", 3, 1)]] + pr[7:8] + load
        + [norm_piece(3, 0), norm_piece(3, 1)] + gu[:2] + stats_pieces(3, [2, 3]) + gu[2:])
    return out + attention_steps(CA, ([] if first else sum(b[BESIDE_MID:], [])) + downs, late, end)


def start_steps():
    pr = project_pieces()
    norms = sum([[[("scale", 1, t)], norm_piece(1, t)] for t in range(T)], [])
    return pipeline(stats_pieces(1, [0, 1, 2, 3]) + norms[:4] + [[("weight_v",)]] + norms[4:]
                    + pr[:2] + [pr[4], pr[2], pr[5], pr[3], pr[6], pr[7]] + [[]]
                    + [[("stack_proj",)], [("tables",)], [("add_bo", 1)]])


def tail_steps():
    return pipeline(
        gate_up_pieces(0, MH - LATER) + [[("scale", 3, 2)], [("scale", 3, 3)]]
        + [norm_piece(3, 2), norm_piece(3, 3), down_piece(0, 0), down_piece(0, 1)]
        + gate_up_pieces(1) + [down_piece(1, 2), down_piece(1, 3)])


def build(nc, x, ctx, ctx_kT, lens, wvT, bv, woT, bo, key_bias, wgT, wuT, wdT, positions, row_consts, out):
    plans = {}
    order = []
    before = 0
    for name, steps, first in (
            ("start", start_steps(), -1),
            ("batch0", batch_steps(True, False), 0),
            ("loop", batch_steps(False, False), 1),
            ("last", batch_steps(False, True), B - 1),
            ("tail", tail_steps(), B)):
        w = Work(steps, before, first)
        plans[name] = (steps, w)
        order.append(name)
        assert w.units % 2 == 0
        before += w.units * (B - 2 if name == "loop" else 1)

    with ExitStack() as es:
        def sb(name, shape, dt):
            return es.enter_context(nc.sbuf_tensor(name, shape, dt))

        def ps(name, shape):
            return es.enter_context(nc.psum_tensor(name, shape, F32))

        def sem(name):
            return es.enter_context(nc.semaphore(name))

        wv = sb("wv", [P, 2, KD, D], F16)
        wo = sb("wo", [P, 2, KD, D], F16)
        wg = sb("wg", [P, KD, HID], F16)
        wu = sb("wu", [P, KD, HID], F16)
        wd = sb("wd", [P, MH, D], F16)
        probs = sb("probs", [P, T, HG, S], F32)
        q_stack = sb("q_stack", [P, G, HG, S], F16)
        k_stack = sb("k_stack", [P, G, HG, S], F16)
        xin = sb("xin", [P, T, D], F32)
        res1 = sb("res1", [P, T, D], F32)
        res2 = sb("res2", [P, T, D], F32)
        xn = sb("xn", [P, 4, D], F32)
        actT = sb("actT", [P, 2, KD, S], F16)
        x3T = sb("x3T", [P, 2, KD, HALF], F16)
        hid = sb("hid", [P, 2, MH, HALF], F16)
        v_self = sb("v_self", [P, T, D], F32)
        v_ctx = sb("v_ctx", [P, T, D], F32)
        pqT = sb("pqT", [P, 2, KD, S], F16)
        keyT = sb("keyT", [P, S], F32)
        bvb = sb("bvb", [P, D], F32)
        bob = sb("bob", [P, D], F32)
        attn_raw = sb("attn_raw", [P, 2, S], F32)
        den = sb("den", [P, S], F32)
        attn_div = sb("attn_div", [P, S], F32)
        th = sb("th", [P, 2, HALF], F32)
        hraw = sb("hraw", [P, 2, HALF], F32)
        shift_row = sb("shift_row", [HG * T, P], F16)
        ident = sb("ident", [P, P], F32)
        ones = sb("ones", [P, DH], F32)
        negmax = sb("negmax", [P, 2, HG * T], F32)
        rcol = sb("rcol", [P, T * HG], F32)
        carrier = sb("carrier", [P, 1], F32)
        carrier_pool = sb("carrier_pool", [P, 1], F32)
        bst = sb("bst", [P, 3, T, 6], F32)
        mv = sb("mv", [P, 3, T, 2], F32)
        rs = sb("rs", [P, 3, T], F32)
        powers = sb("powers", [P, 2, T], F32)
        gate = sb("gate", [P, B], F32)
        lens_i = sb("lens_i", [P, B], I32)
        wv_raw = probs[:, 0]
        wo_raw = probs[:, 1]
        w_raw = hid[:].rearrange("p a m s -> p (a m s)").bitcast(I32).rearrange("p (c n) -> p c n", c=2)
        pos8 = probs[0:B, 2, 0]
        bias8 = probs[0:B, 2, 1]
        inv8 = probs[0:B, 2, 2]
        len8f = probs[0:B, 3, 0, 0:1]
        gate8 = probs[0:B, 3, 0, 1:2]
        len8i = probs[0:B, 3, 1, 0:1].bitcast(I32)
        rows8 = probs[0:B, 3, 2:4].rearrange("p a s -> p (a s)").bitcast(F16).rearrange(
            "p (r s) -> p r s", s=S)[:, 0:3]

        score_b = ps("score_b", [P, 3, S])
        score_a = ps("score_a", [P, 2, S])
        attn = ps("attn", [P, S])
        work = ps("work", [P, 2, S])

        key_rows = nc.dram_tensor("key_rows", [B, 3, S], F16, kind="Internal").ap()

        x_in = sem("x_in")
        xin_in = sem("xin_in")
        v_in = sem("v_in")
        key_in = sem("key_in")
        q_stacked = sem("q_stacked")
        q_first = sem("q_first")
        k_stacked = sem("k_stacked")
        last_stacked = sem("last_stacked")
        shift_in = sem("shift_in")
        stored = sem("stored")
        consts_in = sem("consts_in")
        wraw_in = [sem("wraw_in0"), sem("wraw_in1")]
        rows_out = sem("rows_out")
        row99_in = sem("row99_in")
        consts_made = sem("consts_made")
        table_step = sem("table_step")
        w_hi = sem("w_hi")
        w_lo = sem("w_lo")
        w_int = sem("w_int")
        work_free = [sem("work_free0"), sem("work_free1")]
        stat = {ln: sem(f"stat{ln}") for ln in (1, 2, 3)}
        meanvar = {ln: sem(f"meanvar{ln}") for ln in (1, 2, 3)}
        rstd = {ln: sem(f"rstd{ln}") for ln in (1, 2, 3)}
        normed = {ln: sem(f"normed{ln}") for ln in (1, 2, 3)}
        norm_t = {ln: sem(f"norm_t{ln}") for ln in (1, 2, 3)}
        norm_hi = {ln: sem(f"norm_hi{ln}") for ln in (1, 2, 3)}
        bo_added = sem("bo_added")
        proj_done = sem("proj_done")
        v_made = sem("v_made")
        projt_done = sem("projt_done")
        projt_hi = sem("projt_hi")
        a_filled = sem("a_filled")
        max_done = sem("max_done")
        shift_t = sem("shift_t")
        b_filled = sem("b_filled")
        exp_done = sem("exp_done")
        values_done = sem("values_done")
        attn_out = sem("attn_out")
        sums = sem("sums")
        denom_done = sem("denom_done")
        div_done = sem("div_done")
        div_hi = sem("div_hi")
        div_used = sem("div_used")
        outproj_done = sem("outproj_done")
        key_hi = sem("key_hi")
        key_lo = sem("key_lo")
        back_d = sem("back_d")
        back_o = sem("back_o")
        gu_filled = sem("gu_filled")
        tanh_done = sem("tanh_done")
        silu_done = sem("silu_done")
        hid_hi = sem("hid_hi")
        hid_lo = sem("hid_lo")
        down_done = sem("down_done")
        side_free = sem("side_free")

        Q_PARTS = (0, 0, 1)
        K_PARTS = (0, 1, 0)
        BLOCKS = 16 * 3 * HG
        K_BLOCKS = 2 * BLOCKS + 16 * 4

        def q_ready(x_, at):
            return q_stacked, at.count(2 * BLOCKS, BLOCKS * (1 + x_))

        def k_ready(x_, at):
            return k_stacked, at.count(K_BLOCKS, BLOCKS + 16 if x_ == SA else K_BLOCKS)

        def need(eng, s, value):
            if not isinstance(value, int) or value > 0:
                eng.wait_ge(s, value)

        def claim_raw(eng, x_, g, at):
            u = G * x_ + g
            if (u - 2) % USES < G:
                need(eng, div_done, at.count(G, g - 1 if x_ == SA else G - 1 + g))
            else:
                need(eng, back_o, at.count(G, g - 1 if x_ == CA else g - G + G - 1))
            eng.wait_ge(values_done, at.count(USES * T, T * (u + 1)))

        def walk(eng, do):
            for name in order:
                steps, w = plans[name]
                if name == "loop":
                    with eng.Fori(1, B - 1) as b:
                        for step in steps:
                            do(step, At(b), w)
                else:
                    for step in steps:
                        do(step, At(None, w.first), w)

        def gu_at(hf, m, at):
            return at if hf == 0 and m < MH - LATER else at.plus(-1)

        def ln_at(ln, t, at):
            return at.plus(1) if ln == 1 else at.plus(-1) if ln == 3 and t >= 2 else at

        def side(kind, t, at):
            if at.reg is None and at.off < 0:
                return T * ("norm1", "v").index(kind) + t
            kinds = ("norm2", "norm3") if at.reg is None and at.off == B - 1 else ("norm2", "norm1", "v", "norm3")
            return at.count(4 * T, 2 * T + T * kinds.index(kind) + t)

        def side_before(x_, at):
            if x_ == SA:
                return 2 * T if at.reg is None and at.off == 0 else at.count(4 * T, 2 * T - 2)
            return at.count(4 * T, 3 * T)

        def rstd_ops(ln, tiles):
            ops = 3 if ln == 2 else 2
            per, n = {1: (2, 1), 2: (12, tiles[-1] + 1), 3: (4, tiles[-1] // 2 + 1)}[ln]
            return per, ops * n

        def folded(part, g):
            return actT[:, part, :, P * g:P * (g + 1)].rearrange("p k (j b) -> p j k b", j=HG)

        block = es.enter_context(nc.Block())

        @block.sync
        def _(sp):
            def load_ordered(xb):
                rows = xb.rearrange("(b k j) d -> k b j d", k=KD, j=T)
                for k in range(KD):
                    sp.dma_start(xin[DH * k:DH * (k + 1)], rows[k]).then_inc(xin_in, 16)

            load_ordered(x[0])
            sp.dma_start(wv_raw, wvT.rearrange("(k p) e -> p k e", p=P)).then_inc(wraw_in[0], 16)
            sp.dma_start(bvb[:], bv.rearrange("(o d) -> o d", o=1).broadcast_to([P, D])).then_inc(consts_in, 16)
            sp.dma_start(bob[:], bo.rearrange("(o d) -> o d", o=1).broadcast_to([P, D])).then_inc(consts_in, 16)
            sp.dma_start(pos8, positions.broadcast_to([B, S])).then_inc(consts_in, 16)
            sp.dma_start(bias8, key_bias.rearrange("(o d) -> o d", o=1).broadcast_to([B, S])).then_inc(consts_in, 16)
            sp.dma_start(len8i, lens).then_inc(consts_in, 16)
            sp.dma_start(lens_i[:], lens.rearrange("b o -> o b").broadcast_to([P, B])).then_inc(consts_in, 16)
            sp.dma_start(res1[:], x[0].rearrange("(t p) d -> p t d", p=P)).then_inc(x_in, 16)
            sp.dma_start(wo_raw, woT.rearrange("(k p) e -> p k e", p=P)).then_inc(wraw_in[1], 16)
            sp.dma_start(k_stack[99:100], row_consts[3:4].rearrange("r (g j s) -> r g j s", g=G, j=HG)
                         ).then_inc(row99_in, 16)
            sp.dma_start(v_ctx[:], ctx[0, :, D:2 * D].rearrange("(t p) d -> p t d", p=P)).then_inc(v_in, 16)
            def load_keys(at, g):
                sp.dma_start(keyT[:], ctx_kT[bass.ds(at.index(), 1), P * g:P * (g + 1), :].rearrange(
                    "o e s -> (o e) s")).then_inc(key_in, 16)

            def fill_stack(stack, src, parts, done, groups=range(G), tokens=slice(0, S)):
                a, b = groups[0], groups[-1] + 1
                for j in range(HG):
                    for r, part in enumerate(parts):
                        sp.dma_start(stack[DH * r:DH * (r + 1), a:b, j, tokens],
                                     src[DH * j:DH * (j + 1), part, a:b, tokens]).then_inc(done, 16)

            def do(step, at, w):
                kind = step[0]
                if kind == "tables":
                    sp.wait_ge(table_step, 9)
                    sp.dma_start(key_rows, rows8).then_inc(rows_out, 16)
                    sp.wait_ge(rows_out, 16)
                    load_keys(At(None, 0), 0)
                elif kind == "load_x" and not (at.reg is None and at.off == -1):
                    sp.wait_ge(div_used, at.count(USES, USES))
                    sp.dma_start(res1[:], x[bass.ds(at.plus(1).index(), 1)].rearrange(
                        "o (t p) d -> p (o t) d", p=P)).then_inc(x_in, 16)
                elif kind == "load_ordered" and not (at.reg is None and at.off == -1):
                    sp.wait_ge(normed[1], at.count(T, T))
                    load_ordered(x[bass.ds(at.plus(1).index(), 1)].rearrange("o s d -> (o s) d"))
                elif kind == "load_v":
                    sp.wait_ge(values_done, at.count(USES * T, USES * T))
                    sp.dma_start(v_ctx[:], ctx[bass.ds(at.plus(1).index(), 1), :, D:2 * D].rearrange(
                        "o (t p) d -> p (o t) d", p=P)).then_inc(v_in, 16)
                elif kind == "stack_proj":
                    need(sp, b_filled, at.count(USES * UNITS, USES * UNITS))
                    sp.dma_start(k_stack[96:97], row_consts[0:1].rearrange("r (g j s) -> r g j s", g=G, j=HG)
                                 ).then_inc(k_stacked, 16)
                    sp.wait_ge(side_free, side("v", T - 1, at) + 1)
                    fill_stack(k_stack, pqT, K_PARTS, k_stacked)
                    fill_stack(q_stack, pqT, Q_PARTS, q_stacked)
                elif kind == "shift_row":
                    _, x_, g = step
                    key = ("shift", x_, g)
                    sp.wait_ge(work_free[w.bank(key)], w.released(key, at))
                    row = SHIFT_ROW[x_]
                    sp.dma_start(q_stack[row:row + 1, g, :, :].rearrange(
                        "o j (t s) -> o (j t) s", s=P), shift_row[:, :]).then_inc(shift_in, 16)
                elif kind == "keys":
                    g = step[1]
                    sp.wait_ge(key_lo, at.count(G, g + 1))
                    nb, ng = (at, g + 1) if g + 1 < G else (at.plus(1), 0)
                    if nb.reg is not None or nb.off < B:
                        load_keys(nb, ng)
                elif kind == "stack_keys":
                    groups = step[1]
                    sp.wait_ge(b_filled, at.count(USES * UNITS, (groups[-1] + 1) * UNITS))
                    sp.wait_ge(key_lo, at.count(G, groups[-1] + 1))
                    done = last_stacked if groups[-1] == G - 1 else k_stacked
                    fill_stack(k_stack, pqT, K_PARTS, done, groups)
                    for g in groups:
                        sp.dma_start(k_stack[96:99, g, :, :], key_rows[bass.ds(at.index(), 1)].rearrange(
                            "o r s -> (o r) s").unsqueeze(1).broadcast_to([3, HG, S])).then_inc(done, 16)
                elif kind == "queries":
                    half = step[1]
                    tokens = slice(HALF * half, HALF * (half + 1))
                    if half == 0:
                        sp.wait_ge(b_filled, at.count(USES * UNITS, G * UNITS))
                    sp.wait_ge(side_free, side("norm2", 2 * half + 1, at) + 1)
                    if half == 0:
                        sp.dma_start(q_stack[96:99], row_consts[0:3].rearrange("r (g j s) -> r g j s", g=G, j=HG)
                                     ).then_inc(q_first, 16)
                    fill_stack(q_stack, actT, Q_PARTS, (q_first, q_stacked)[half], tokens=tokens)
                elif kind == "down_add":
                    _, hf, t = step
                    key = ("down", hf, t)
                    sp.wait_ge(work_free[w.bank(key)], w.released(key, at))
                    sp.dma_start(out.rearrange("b s d -> (b s) d")[bass.ds(at.plus(-1).count(S, P * t), P), :],
                                 res2[:, t, :]).then_inc(stored, 16)
                elif kind == "weights":
                    c = step[1]
                    need(sp, w_int, c - 1)
                    src, k = divmod(c, KD)
                    if src < 2:
                        sp.dma_start(w_raw[:, c % 2], (wgT, wuT)[src][P * k:P * (k + 1), :]
                                     ).then_inc(wraw_in[c % 2], 16)
                    else:
                        sp.dma_start(w_raw[:, c % 2].rearrange("p (m n) -> p m n", n=D),
                                     wdT[3 * P * k:3 * P * (k + 1), :].rearrange("(m p) n -> p m n", p=P)
                                     ).then_inc(wraw_in[c % 2], 16)
            walk(sp, do)
            sp.wait_ge(stored, 16 * T * B)
            sp.wait_ge(rows_out, 16)

        @block.tensor
        def _(pe):
            pe.wait_ge(consts_made, 6)
            pe.wait_ge(row99_in, 16)

            def do(step, at, w):
                kind = step[0]

                def claim(key):
                    need(pe, work_free[w.bank(key)], w.free(key, at))
                    return work[:, w.bank(key), :]

                def claim_side(kind_, t):
                    before = kind_ == "norm3" and t >= 2
                    need(pe, side_free, side(kind_, t, at.plus(-1) if before else at) - 1)
                    if at.reg is None and at.off == B:
                        pe.wait_ge(max_done, B * USES * UNITS)
                    elif at.reg is not None or at.off >= 0:
                        phases = 1 if before or kind_ == "norm2" else 2
                        pe.wait_ge(max_done, at.count(USES * UNITS, G * UNITS * phases))
                    return score_a[:, t % 2, :]

                def written(keys, claimed):
                    last = {w.bank(k): k for k in keys}
                    for bank, k in last.items():
                        if bank != w.bank(claimed):
                            pe.wait_ge(work_free[bank], w.released(k, at))

                if kind == "norm":
                    _, ln, t = step
                    bank = claim_side(f"norm{ln}", t)
                    la = ln_at(ln, t, at)
                    pe.wait_ge(normed[ln], la.count(T, t + 1))
                    for k in range(KD):
                        last = nc.tensor.transpose(bank[:, P * k:P * (k + 1)],
                                                   xn[:, t % 2 + 2 * (ln == 3), P * k:P * (k + 1)], ident[:])
                    last.then_inc(norm_t[ln], 1)
                elif kind == "proj":
                    t = step[1]
                    bank = claim(step)
                    if t == 0:
                        need(pe, w_lo, 1)
                    pe.wait_ge(side_free, side("norm1", t, at) + 1)
                    n = 0
                    for k in range(KD):
                        for a, c in ((0, 0), (0, 1), (1, 0)):
                            last = nc.tensor.matmul(bank, actT[:, a, k, P * t:P * (t + 1)], wv[:, c, k, :],
                                                    start=n == 0, stop=n == 3 * KD - 1)
                            n += 1
                    last.then_inc(proj_done, 1)
                elif kind == "proj_t":
                    t = step[1]
                    bank = claim_side("v", t)
                    pe.wait_ge(v_made, at.plus(1).count(T, t + 1))
                    for g in range(G):
                        last = nc.tensor.transpose(bank[:, P * g:P * (g + 1)], v_self[:, t, P * g:P * (g + 1)],
                                                   ident[:])
                    last.then_inc(projt_done, 1)
                elif kind == "maxima":
                    _, x_, a = step
                    g, t, j = a // UNITS, a % UNITS // HG, a % HG
                    n = G * UNITS * x_ + a
                    if a == 0 and x_ == CA:
                        pe.wait_ge(q_first, at.count(BLOCKS + 16, BLOCKS + 16))
                    if a == (0 if x_ == SA else 2 * HG):
                        pe.wait_ge(*q_ready(x_, at))
                    if a == 0:
                        pe.wait_ge(*k_ready(x_, at))
                        need(pe, side_free, side_before(x_, at))
                    if a == 3 * UNITS and x_ == CA:
                        pe.wait_ge(last_stacked, at.count(BLOCKS + 16, BLOCKS + 16))
                    need(pe, max_done, at.count(USES * UNITS, n - 1))
                    nc.tensor.matmul(score_a[:, n % 2, :], q_stack[0:K_MAX[x_], g, j, P * t:P * (t + 1)],
                                     k_stack[0:K_MAX[x_], g, j, :], start=True, stop=True).then_inc(a_filled, 1)
                elif kind == "shift":
                    _, x_, g = step
                    u = G * x_ + g
                    bank = claim(step)
                    pe.wait_ge(max_done, at.count(USES * UNITS, (u + 1) * UNITS))
                    nc.tensor.transpose(bank[0:HG * T, 0:P], negmax[:, g % 2, :], ident[:]).then_inc(shift_t, 1)
                elif kind == "probs":
                    _, x_, n = step
                    g, kt, j = n // UNITS, n % UNITS // HG, n % HG
                    n += G * UNITS * x_
                    rows = SHIFT_ROW[x_] + 1
                    if n % UNITS == 0:
                        pe.wait_ge(shift_in, at.count(16 * USES, 16 * (n // UNITS + 1)))
                    need(pe, exp_done, at.count(USES * UNITS, n - 2 if n > 1 else n - 1))
                    nc.tensor.matmul(score_b[:, n % 3, :], k_stack[0:rows, g, j, P * kt:P * (kt + 1)],
                                     q_stack[0:rows, g, j, :], start=True, stop=True).then_inc(b_filled, 1)
                elif kind == "values":
                    _, x_, g, kt = step
                    u = G * x_ + g
                    v = v_self if x_ == SA else v_ctx
                    if kt == 0:
                        need(pe, attn_out, at.count(USES, u))
                        if x_ == CA and g == 0:
                            pe.wait_ge(v_in, at.count(16, 16))
                    pe.wait_ge(exp_done, at.count(USES * UNITS, u * UNITS + (kt + 1) * HG))
                    for j in range(HG):
                        h = g * HG + j
                        if x_ == CA:
                            last = nc.tensor.matmul(attn[DH * j:DH * (j + 1), :], v[:, kt, DH * h:DH * (h + 1)],
                                                    probs[:, kt, j, :], start=kt == 0, stop=kt == T - 1)
                        else:
                            for i in range(T):
                                last = nc.tensor.matmul(attn[DH * i:DH * (i + 1), P * j:P * (j + 1)],
                                                        v[:, kt, DH * h:DH * (h + 1)],
                                                        probs[:, kt, j, P * i:P * (i + 1)],
                                                        start=kt == 0 and j == 0, stop=kt == T - 1 and j == HG - 1,
                                                        skip_group_check=True)
                    last.then_inc(values_done, 1)
                elif kind == "denom":
                    _, x_, g, parts = step
                    u = G * x_ + g
                    key = ("denom", x_, g)
                    bank = work[:, w.bank(key), :]
                    for half in parts:
                        if half == 0:
                            claim(key)
                        pe.wait_ge(sums, at.count(4 * USES, 4 * u + 2 + 2 * half))
                        slot = 1 + 2 * half
                        for i in range(HG):
                            summed = probs[:, slot, i, :] if x_ == CA else probs[:, slot, :, P * i:P * (i + 1)]
                            last = nc.tensor.matmul(bank[DH * i:DH * (i + 1), :], ones[:], summed,
                                                    start=half == 0, stop=half == 1)
                        last.then_inc(denom_done, 1)
                elif kind == "back_d":
                    g = step[1]
                    bank = claim(step)
                    written([("denom", CA, g)], step)
                    for t in range(T):
                        last = nc.tensor.transpose(bank[:, P * t:P * (t + 1)], den[:, P * t:P * (t + 1)], ident[:])
                    last.then_inc(back_d, 1)
                elif kind == "back_o":
                    g = step[1]
                    bank = claim(step)
                    pe.wait_ge(attn_out, at.count(USES, G + g + 1))
                    for t in range(T):
                        last = nc.tensor.transpose(bank[:, P * t:P * (t + 1)],
                                                   attn_raw[:, g % 2, P * t:P * (t + 1)], ident[:])
                    last.then_inc(back_o, 1)
                elif kind == "out_proj":
                    t = step[1]
                    bank = claim(step)
                    pe.wait_ge(div_used, at.count(USES, t + 1))
                    if t == 0:
                        need(pe, w_lo, 2)
                    n = 0
                    for k in range(KD):
                        for a, c in ((0, 0), (0, 1), (1, 0)):
                            last = nc.tensor.matmul(bank, actT[:, a, k, P * t:P * (t + 1)], wo[:, c, k, :],
                                                    start=n == 0, stop=n == 3 * KD - 1)
                            n += 1
                    last.then_inc(outproj_done, 1)
                elif kind == "gate_up":
                    _, hf, m = step
                    bank = claim(step)
                    if m == 0:
                        pe.wait_ge(side_free, side("norm3", 2 * hf + 1, gu_at(hf, m, at)) + 1)
                        need(pe, w_int, 2 * KD)
                    for half, wt in enumerate((wg, wu)):
                        for k in range(KD):
                            for a in (0, 1):
                                last = nc.tensor.matmul(bank[:, HALF * half:HALF * (half + 1)], wt[:, k, P * m:P * (m + 1)],
                                                        x3T[:, a, k, :], start=k == 0 and a == 0, stop=k == KD - 1 and a == 1)
                    last.then_inc(gu_filled, 1)
                elif kind == "down":
                    _, hf, t, parts = step
                    key = ("down", hf, t)
                    bank = work[:, w.bank(key), :]
                    ma = at.plus(-1)
                    if parts[0] == 0:
                        claim(key)
                        if hf == 0 and t == 0:
                            need(pe, w_int, 3 * KD)
                    tt = t - 2 * hf
                    for m in parts:
                        if t % 2 == 0 and m in (0, MH - 2):
                            pe.wait_ge(hid_lo, ma.count(2 * MH, MH * hf + (m or MH - 2) + 2 * (m > 0)))
                        for a in (0, 1):
                            last = nc.tensor.matmul(bank, hid[:, a, m, P * tt:P * (tt + 1)], wd[:, m, :],
                                                    start=m == 0 and a == 0, stop=m == MH - 1 and a == 1)
                    if parts[-1] == MH - 1:
                        last.then_inc(down_done, 1)
            walk(pe, do)

        @block.scalar
        def _(act):
            def weight_hi(n, raw, parts):
                act.wait_ge(wraw_in[n], 16)
                nc.scalar.activation(parts[:, 0], raw, ACT.Copy, scale=SW).then_inc(w_hi, 1)

            weight_hi(0, wv_raw, wv)

            def do(step, at, w):
                kind = step[0]
                if kind == "tables":
                    weight_hi(1, wo_raw, wo)
                elif kind == "norm":
                    _, ln, t = step
                    la = ln_at(ln, t, at)
                    act.wait_ge(norm_t[ln], la.count(T, t + 1))
                    src = score_a[:, t % 2, :].rearrange("p (k s) -> p k s", k=KD)
                    if ln == 3:
                        dst = x3T[:, 0, :, P * (t % 2):P * (t % 2 + 1)]
                    else:
                        dst = actT[:, 0, :, P * t:P * (t + 1)]
                    nc.scalar.activation(dst, src, ACT.Copy, scale=SX).then_inc(norm_hi[ln], 1)
                elif kind == "proj_t":
                    t = step[1]
                    act.wait_ge(projt_done, at.plus(1).count(T, t + 1))
                    nc.scalar.activation(pqT[:, 0, :, P * t:P * (t + 1)],
                                         score_a[:, t % 2, :].rearrange("p (k s) -> p k s", k=KD), ACT.Copy,
                                         scale=SP_).then_inc(projt_hi, 1)
                elif kind == "shift_row":
                    _, x_, g = step
                    u = G * x_ + g
                    key = ("shift", x_, g)
                    need(act, shift_in, at.count(16 * USES, 16 * u))
                    act.wait_ge(shift_t, at.count(USES, u + 1))
                    nc.scalar.activation(shift_row[:], work[0:HG * T, w.bank(key), 0:P], ACT.Copy,
                                         scale=1.0 / (SHIFT_SA, SHIFT_CA)[x_]).then_inc(work_free[w.bank(key)], 1)
                elif kind == "probs":
                    _, x_, n = step
                    kt, j = n % UNITS // HG, n % HG
                    n += G * UNITS * x_
                    u = n // UNITS
                    if kt % 2 == 0 and j % 2 == 0:
                        need(act, sums, at.count(4 * USES, 4 * (u - 1) + kt + j // 2 + 1))
                    elif kt % 2 and j == 0:
                        need(act, denom_done, at.count(2 * USES, 2 * (u - 1) + 1 + kt // 2))
                    act.wait_ge(b_filled, at.count(USES * UNITS, n + 1))
                    nc.scalar.activation(probs[:, kt, j, :], score_b[:, n % 3, :], ACT.Exp,
                                         scale=(1.0 / (SP_ * SP_ * DH ** 0.5), 1.0 / CA_SCORE)[x_]).then_inc(exp_done, 1)
                elif kind == "evacuate" and step[2] < 2:
                    _, x_, g = step
                    claim_raw(act, x_, g, at)
                    nc.scalar.activation(attn_raw[:, g % 2, :], attn[:], ACT.Copy,
                                         scale=(SP_, 1.0)[x_]).then_inc(attn_out, 1)
                elif kind == "den_copy":
                    g = step[1]
                    key = ("denom", CA, g)
                    act.wait_ge(denom_done, at.count(2 * USES, 2 * (G + g + 1)))
                    need(act, back_d, at.count(G, g))
                    nc.scalar.activation(den[:], work[:, w.bank(key), :], ACT.Copy).then_inc(work_free[w.bank(key)], 1)
                elif kind == "fold":
                    g = step[1]
                    act.wait_ge(div_done, at.count(G, g + 1))
                    nc.scalar.activation(folded(0, g), attn_div[:].rearrange("p (j k b) -> p j k b", j=HG, k=KD),
                                         ACT.Copy).then_inc(div_hi, 1)
                elif kind == "keys":
                    g = step[1]
                    act.wait_ge(key_in, at.count(16 * G, 16 * (g + 1)))
                    if g == 0:
                        act.wait_ge(*q_ready(SA, at))
                        act.wait_ge(*k_ready(SA, at))
                    nc.scalar.activation(pqT[:, 0, g, :], keyT[:], ACT.Copy, scale=SP_).then_inc(key_hi, 1)
                elif kind == "silu":
                    _, hf, m = step
                    ma = gu_at(hf, m, at)
                    act.wait_ge(gu_filled, ma.count(2 * MH, MH * hf + m + 1))
                    nc.scalar.activation(th[:, m % 2, :], work[:, w.bank(("gate_up", hf, m)), 0:HALF], ACT.Tanh,
                                         scale=0.5 * DEQ / SX).then_inc(tanh_done, 1)
                elif kind == "hidden":
                    _, hf, m = step
                    key = ("gate_up", hf, m)
                    act.wait_ge(work_free[w.bank(key)], w.released(key, at))
                    nc.scalar.activation(hid[:, 0, m, :], hraw[:, m % 2, :], ACT.Copy).then_inc(hid_hi, 1)
                elif kind == "to_half":
                    c = step[1]
                    act.wait_ge(wraw_in[c % 2], 16 + 16 * (c // 2 + 1))
                    src, k = divmod(c, KD)
                    dst = (wg[:, k, :], wu[:, k, :], wd[:, 3 * k:3 * (k + 1), :].rearrange("p m n -> p (m n)"))[src]
                    nc.scalar.activation(dst, w_raw[:, c % 2], ACT.Copy).then_inc(w_int, 1)
            walk(act, do)

        @block.vector
        def _(dve):
            def weight_lo(n, raw, parts):
                dve.wait_ge(w_hi, n + 1)
                nc.vector.scalar_tensor_tensor(parts[:, 1].rearrange("p k e -> p (k e)"), raw.rearrange("p k e -> p (k e)"),
                                               SW, parts[:, 0].rearrange("p k e -> p (k e)"),
                                               ALU.mult, ALU.subtract).then_inc(w_lo, 1)

            def make_tables():
                nc.vector.tensor_copy(len8f, len8i).then_inc(table_step, 1)
                dve.wait_ge(table_step, 1)
                nc.vector.tensor_scalar(gate8, len8f, 0.0, None, ALU.is_gt).then_inc(table_step, 1)
                dve.wait_ge(table_step, 2)
                nc.vector.tensor_scalar(inv8, pos8, len8f, gate8, ALU.is_ge, ALU.mult).then_inc(table_step, 1)
                dve.wait_ge(table_step, 3)
                nc.vector.tensor_scalar(rows8[:, 2], inv8, -65504.0, None, ALU.mult).then_inc(table_step, 1)
                nc.vector.tensor_scalar(bias8, bias8, gate8, SP_, ALU.mult, ALU.mult).then_inc(table_step, 1)
                dve.wait_ge(table_step, 5)
                nc.vector.tensor_copy(rows8[:, 0], bias8).then_inc(table_step, 1)
                dve.wait_ge(table_step, 6)
                nc.vector.tensor_tensor(rows8[:, 1], bias8, rows8[:, 0], ALU.subtract).then_inc(table_step, 1)
                nc.vector.tensor_copy(gate[:], lens_i[:]).then_inc(table_step, 1)
                dve.wait_ge(table_step, 8)
                nc.vector.tensor_scalar(gate[:], gate[:], 0.0, DH ** -0.5, ALU.is_gt, ALU.mult).then_inc(table_step, 1)

            def do(step, at, w):
                kind = step[0]
                if kind == "weight_v":
                    dve.wait_ge(consts_in, 16 * 6)
                    weight_lo(0, wv_raw, wv)
                elif kind == "tables":
                    weight_lo(1, wo_raw, wo)
                    make_tables()
                elif kind == "stats":
                    _, ln, t = step
                    la = at.plus(1) if ln == 1 else at
                    if ln == 1:
                        dve.wait_ge(xin_in, la.count(16 * KD, 16 * KD))
                        src = xin
                    elif ln == 2:
                        key = ("out_proj", t)
                        dve.wait_ge(work_free[w.bank(key)], w.released(key, at))
                        src = res1
                    else:
                        dve.wait_ge(div_used, la.count(USES, USES))
                        src = res2
                    nc.vector.bn_stats(bst[:, ln - 1, t, :], src[:, t, :]).then_inc(stat[ln], 1)
                elif kind == "rstd":
                    _, ln, tiles = step
                    la = at.plus(1) if ln == 1 else at
                    dve.wait_ge(stat[ln], la.count(T, tiles[-1] + 1))
                    nc.vector.memset(carrier[:], 0.0)
                    for t in tiles:
                        nc.vector.bn_aggr(mv[:, ln - 1, t, :], bst[:, ln - 1, t, :]).then_inc(meanvar[ln], 1)
                elif kind == "scale":
                    _, ln, t = step
                    la = ln_at(ln, t, at)
                    dve.wait_ge(rstd[ln], la.count(*rstd_ops(ln, (3,) if ln == 1 else (t,))))
                    if t >= 2:
                        dve.wait_ge(norm_t[ln], la.count(T, t - 1))
                    nc.vector.tensor_scalar(xn[:, t % 2 + 2 * (ln == 3), :], (xin, res1, res2)[ln - 1][:, t, :],
                                            mv[:, ln - 1, t, 0:1], rs[:, ln - 1, t:t + 1],
                                            ALU.subtract, ALU.mult).then_inc(normed[ln], 1)
                elif kind == "norm_lo":
                    _, ln, t = step
                    la = ln_at(ln, t, at)
                    dve.wait_ge(norm_hi[ln], la.count(T, t + 1))
                    src = score_a[:, t % 2, :].rearrange("p (k s) -> p k s", k=KD)
                    buf, col = (x3T, t % 2) if ln == 3 else (actT, t)
                    nc.vector.scalar_tensor_tensor(buf[:, 1, :, P * col:P * (col + 1)], src, SX,
                                                   buf[:, 0, :, P * col:P * (col + 1)],
                                                   ALU.mult, ALU.subtract).then_inc(side_free, 1)
                elif kind == "proj_add":
                    t = step[1]
                    bank = w.bank(("proj", t))
                    dve.wait_ge(proj_done, at.plus(1).count(T, t + 1))
                    nc.vector.scalar_tensor_tensor(v_self[:, t, :], work[:, bank, :], 1.0 / (SX * SW), bvb[:],
                                                   ALU.mult, ALU.add).then_inc(work_free[bank], 1)
                    dve.wait_ge(work_free[bank], w.released(("proj", t), at))
                    nc.vector.memset(carrier[:], 0.0).then_inc(v_made, 1)
                elif kind == "proj_lo":
                    t = step[1]
                    dve.wait_ge(projt_hi, at.plus(1).count(T, t + 1))
                    nc.vector.scalar_tensor_tensor(pqT[:, 1, :, P * t:P * (t + 1)],
                                                   score_a[:, t % 2, :].rearrange("p (k s) -> p k s", k=KD), SP_,
                                                   pqT[:, 0, :, P * t:P * (t + 1)],
                                                   ALU.mult, ALU.subtract).then_inc(side_free, 1)
                elif kind == "maxima":
                    _, x_, a = step
                    g, t, j = a // UNITS, a % UNITS // HG, a % HG
                    n = G * UNITS * x_ + a
                    if a % UNITS == 0:
                        need(dve, shift_t, at.count(USES, n // UNITS - 1))
                    dve.wait_ge(a_filled, at.count(USES * UNITS, n + 1))
                    nc.vector.tensor_reduce(negmax[:, g % 2, T * j + t:T * j + t + 1], score_a[:, n % 2, :], AX_X, ALU.max,
                                            negate=True).then_inc(max_done, 1)
                elif kind == "evacuate" and step[2] >= 2:
                    _, x_, g = step
                    claim_raw(dve, x_, g, at)
                    nc.vector.tensor_scalar(attn_raw[:, g % 2, :], attn[:], (SP_, 1.0)[x_], None,
                                            ALU.mult).then_inc(attn_out, 1)
                elif kind == "divide":
                    _, g, quarters = step
                    bank = w.bank(("denom", SA, g))
                    if quarters[0] == 0:
                        need(dve, div_done, at.count(G, g))
                        dve.wait_ge(denom_done, at.count(2 * USES, 2 * (g + 1)))
                    for q in quarters:
                        last = nc.vector.reciprocal(den[:, P * q:P * (q + 1)], work[:, bank, P * q:P * (q + 1)])
                    if q == T - 1:
                        last.then_inc(work_free[bank], 1)
                elif kind == "back_r":
                    g = step[1]
                    bank = w.bank(("back_d", g))
                    dve.wait_ge(back_d, at.count(G, g + 1))
                    nc.vector.reciprocal(rcol[:], work[:, bank, :].rearrange("p (n i) -> p n i", i=DH)[:, :, 0]
                                         ).then_inc(work_free[bank], 1)
                elif kind == "back_add":
                    g = step[1]
                    kd, ko = ("back_d", g), ("back_o", g)
                    dve.wait_ge(back_o, at.count(G, g + 1))
                    dve.wait_ge(work_free[w.bank(kd)], w.released(kd, at))
                    need(dve, div_used, at.count(USES, G + g))
                    nc.vector.tensor_tensor(attn_div[:].rearrange("p (n i) -> p n i", i=DH),
                                            work[:, w.bank(ko), :].rearrange("p (n i) -> p n i", i=DH),
                                            rcol[:].unsqueeze(2).broadcast_to([P, T * HG, DH]),
                                            ALU.mult).then_inc(work_free[w.bank(ko)], 1)
                elif kind == "out_add":
                    t = step[1]
                    bank = w.bank(("out_proj", t))
                    dve.wait_ge(outproj_done, at.count(T, t + 1))
                    if t == 0:
                        dve.wait_ge(bo_added, at.count(1, 1))
                    nc.vector.scalar_tensor_tensor(res1[:, t, :], work[:, bank, :], 1.0 / (SP_ * SW), res1[:, t, :],
                                                   ALU.mult, ALU.add).then_inc(work_free[bank], 1)
                elif kind == "keys":
                    g = step[1]
                    dve.wait_ge(key_hi, at.count(G, g + 1))
                    nc.vector.scalar_tensor_tensor(pqT[:, 1, g, :], keyT[:], SP_, pqT[:, 0, g, :],
                                                   ALU.mult, ALU.subtract).then_inc(key_lo, 1)
                elif kind == "silu":
                    _, hf, m = step
                    ma = gu_at(hf, m, at)
                    n = MH * hf + m
                    bank = work[:, w.bank(("gate_up", hf, m)), :]
                    dve.wait_ge(tanh_done, ma.count(2 * MH, n + 1))
                    nc.vector.scalar_tensor_tensor(th[:, m % 2, :], th[:, m % 2, :], 1.0, bank[:, 0:HALF],
                                                   ALU.add, ALU.mult).then_inc(silu_done, 1)
                    dve.wait_ge(silu_done, ma.count(2 * MH, n + 1))
                    need(dve, hid_lo, ma.count(2 * MH, n - 1))
                    nc.vector.scalar_tensor_tensor(hraw[:, m % 2, :], th[:, m % 2, :], 0.5 * SHID * (DEQ / SX) ** 2,
                                                   bank[:, HALF:2 * HALF], ALU.mult, ALU.mult
                                                   ).then_inc(work_free[w.bank(("gate_up", hf, m))], 1)
                elif kind == "down_add":
                    _, hf, t = step
                    bank = w.bank(("down", hf, t))
                    dve.wait_ge(down_done, at.plus(-1).count(T, t + 1))
                    nc.vector.scalar_tensor_tensor(res2[:, t, :], work[:, bank, :], DEQ / SHID, res2[:, t, :],
                                                   ALU.mult, ALU.add).then_inc(work_free[bank], 1)
            walk(dve, do)

        @block.gpsimd
        def _(pool):
            nc.gpsimd.memset(ident[:], 0.0).then_inc(consts_made, 1)
            pool.wait_ge(consts_made, 1)
            nc.gpsimd.affine_select(out=ident[:], in_=ident[:], compare_op=ALU.not_equal, fill=1.0, base=0,
                                    pattern=[[-1, P]], channel_multiplier=1).then_inc(consts_made, 1)
            nc.gpsimd.memset(ones[:], 1.0).then_inc(consts_made, 1)
            nc.gpsimd.memset(powers[:, 0, :], EPS).then_inc(consts_made, 1)
            nc.gpsimd.memset(powers[:, 1, :], -0.5).then_inc(consts_made, 1)
            nc.gpsimd.memset(rcol[:], 1.0).then_inc(consts_made, 1)
            pool.wait_ge(consts_made, 6)

            def do(step, at, w):
                kind = step[0]
                if kind == "rstd":
                    _, ln, tiles = step
                    a, b = tiles[0], tiles[-1] + 1
                    la = at.plus(1) if ln == 1 else at
                    per, n = rstd_ops(ln, tiles)
                    n -= 3 if ln == 2 else 2
                    r = rs[:, ln - 1, a:b]
                    pool.wait_ge(meanvar[ln], la.count(T, b))
                    nc.gpsimd.tensor_tensor(r, mv[:, ln - 1, a:b, 1], powers[:, 0, a:b], ALU.add).then_inc(rstd[ln], 1)
                    pool.wait_ge(rstd[ln], la.count(per, n + 1))
                    nc.gpsimd.tensor_tensor(r, r, powers[:, 1, a:b], ALU.pow).then_inc(rstd[ln], 1)
                    if ln == 2:
                        pool.wait_ge(rstd[ln], la.count(per, n + 2))
                        if at.reg is None and at.off == 0:
                            pool.wait_ge(table_step, 9)
                        nc.gpsimd.tensor_tensor(carrier_pool[:], powers[:, 0, 0:1], powers[:, 1, 0:1], ALU.add)
                        nc.gpsimd.tensor_tensor(r, r, gate[:, bass.ds(at.index(), 1)],
                                                ALU.mult).then_inc(rstd[ln], 1)
                elif kind == "add_bo":
                    la = at.plus(step[1])
                    pool.wait_ge(x_in, la.count(16, 16))
                    if at.reg is None and at.off == -1:
                        pool.wait_ge(consts_in, 16 * 6)
                    nc.gpsimd.tensor_tensor(res1[:], res1[:], bob[:].unsqueeze(1).broadcast_to([P, T, D]),
                                            ALU.add).then_inc(bo_added, 1)
                elif kind == "values" and step[3] % 2:
                    _, x_, g, kt = step
                    u = G * x_ + g
                    pool.wait_ge(values_done, at.count(USES * T, T * u + kt + 1))
                    for j in (0, 2):
                        nc.gpsimd.tensor_tensor(probs[:, kt, j:j + 2], probs[:, kt - 1, j:j + 2],
                                                probs[:, kt, j:j + 2], ALU.add).then_inc(sums, 1)
                elif kind == "divide" and step[2][-1] == T - 1:
                    g = step[1]
                    key = ("denom", SA, g)
                    pool.wait_ge(work_free[w.bank(key)], w.released(key, at))
                    pool.wait_ge(attn_out, at.count(USES, g + 1))
                    need(pool, div_used, at.count(USES, g))
                    nc.gpsimd.tensor_tensor(attn_div[:], attn_raw[:, g % 2, :], den[:], ALU.mult).then_inc(div_done, 1)
                elif kind == "fold":
                    g = step[1]
                    pool.wait_ge(div_hi, at.count(G, g + 1))
                    nc.gpsimd.tensor_tensor(folded(1, g), attn_div[:].rearrange("p (j k b) -> p j k b", j=HG, k=KD),
                                            folded(0, g),
                                            ALU.subtract).then_inc(div_used, 1)
                elif kind == "back_add":
                    g = step[1]
                    key = ("back_o", g)
                    if g == 0:
                        need(pool, stored, at.count(16 * T, 0))
                    pool.wait_ge(work_free[w.bank(key)], w.released(key, at))
                    nc.gpsimd.tensor_tensor(res2[:, :, P * g:P * (g + 1)], res1[:, :, P * g:P * (g + 1)],
                                            attn_div[:].rearrange("p (t e) -> p t e", t=T),
                                            ALU.add).then_inc(div_used, 1)
                elif kind == "hidden":
                    _, hf, m = step
                    pool.wait_ge(hid_hi, gu_at(hf, m, at).count(2 * MH, MH * hf + m + 1))
                    nc.gpsimd.tensor_tensor(hid[:, 1, m, :], hraw[:, m % 2, :], hid[:, 0, m, :],
                                            ALU.subtract).then_inc(hid_lo, 1)
            walk(pool, do)


def kernel(x, ctx_2048, itok_Bx1_68_817, L0_attn_Wv, L0_attn_bv, L0_attn_Wo, L0_attn_bo, L0_xattn_b,
           L0_ffn_w_gate, L0_ffn_w_up, L0_ffn_w_down):
    import concourse.bacc as bacc
    from concourse.bass_utils import run_bass_kernel_spmd

    ctx = np.ascontiguousarray(ctx_2048)
    arrays = {
        "x": np.ascontiguousarray(x),
        "ctx": ctx,
        "ctx_kT": np.ascontiguousarray(ctx[:, :, :D].transpose(0, 2, 1)),
        "lens": np.ascontiguousarray(itok_Bx1_68_817),
        "wvT": np.ascontiguousarray(np.asarray(L0_attn_Wv).T),
        "bv": np.ascontiguousarray(L0_attn_bv),
        "woT": np.ascontiguousarray(np.asarray(L0_attn_Wo).T),
        "bo": np.ascontiguousarray(L0_attn_bo),
        "key_bias": np.ascontiguousarray(L0_xattn_b),
        "wgT": np.ascontiguousarray(np.asarray(L0_ffn_w_gate).T),
        "wuT": np.ascontiguousarray(np.asarray(L0_ffn_w_up).T),
        "wdT": np.ascontiguousarray(np.asarray(L0_ffn_w_down).T),
        "positions": np.arange(S, dtype=np.float32)[None, :],
        "row_consts": np.repeat(np.array([[1024.0], [1024.0], [32768.0], [16384.0]], np.float16), H * S, axis=1),
    }
    nc = bacc.Bacc("TRN2", target_bir_lowering=False, num_devices=1,
                   dynamic_dma_scratch_size=1024)
    args = [nc.dram_tensor(f"in_{n}", a.shape, mybir.dt.from_np(a.dtype), kind="ExternalInput").ap()
            for n, a in arrays.items()]
    out = nc.dram_tensor("out", (B, S, D), F32, kind="ExternalOutput").ap()
    build(nc, *args, out)
    r = run_bass_kernel_spmd(nc, [{f"in_{n}": a for n, a in arrays.items()}], core_ids=[0])
    return r.results[0]["out"]
```
